# Optimizing a Trainium2 kernel written in Bass

```python
import numpy as np
import jax
import jax.numpy as jnp

def _softmax(x, axis=-1):
    return jax.nn.softmax(x, axis=axis)

def _gelu(x):
    return jax.nn.gelu(x, approximate=True)

def _silu(x):
    return jax.nn.silu(x)

def _sigmoid(x):
    return jax.nn.sigmoid(x)

def _layernorm(x, axis=-1, eps=1e-05):
    m = jnp.mean(x, axis=axis, keepdims=True)
    v = jnp.var(x, axis=axis, keepdims=True)
    return (x - m) / jnp.sqrt(v + eps)

def _scatter_add(tgt, idx, src, axis=0):
    return tgt.at[idx].add(src)

def _segment_sum(src, seg, n):
    return jax.ops.segment_sum(src, seg, n)
kernel_name = 'mk_adj_resnorm_d1_adj_r2_15dd5a'

def setup_inputs(seed: int=0):
    np.random.seed(seed)
    _w = jnp.asarray

    def _rec_inputs():
        import jax
        import jax.numpy as jnp
        _gk = jax.random.key(seed)
        x = -1.394e-06 + 0.9999 * jax.random.normal(jax.random.fold_in(_gk, 1), (4096, 256), jnp.float32)
        _a = jax.random.bernoulli(jax.random.fold_in(_gk, 2), 0.00390625, (4096, 4096))
        _a = jnp.logical_or(_a, jnp.swapaxes(_a, -1, -2))
        _a = jnp.logical_or(_a, jnp.eye(4096, dtype=bool))
        adj = _a
        return (x, adj)
    x, adj = _rec_inputs()

    def _L0_gnn_setup():
        import jax, jax.numpy as jnp
        import numpy as np
        import math
        N = 4096
        D_IN = 256
        LOCAL_D = 256
        GLOBAL_D = 256
        key = jax.random.key(seed)
        ks = jax.random.split(key, 16)
        s = 1.0 / math.sqrt(D_IN)
        adj = jax.random.bernoulli(ks[0], 0.01, (N, N))
        adj = adj | jnp.eye(N, dtype=bool)
        return {'adj_matrix': adj, 'x': jax.random.normal(ks[1], (N, D_IN), jnp.float32), 'masked_x': jax.random.normal(ks[2], (N, D_IN), jnp.float32), 'Wlq': jax.random.normal(ks[3], (D_IN, LOCAL_D), jnp.float32) * s, 'Wlk': jax.random.normal(ks[4], (D_IN, LOCAL_D), jnp.float32) * s, 'Wlv': jax.random.normal(ks[5], (D_IN, D_IN), jnp.float32) * s, 'blv': jax.random.normal(ks[6], (D_IN,), jnp.float32) * 0.01, 'Wgq': jax.random.normal(ks[7], (D_IN, GLOBAL_D), jnp.float32) * s, 'Wgk': jax.random.normal(ks[8], (D_IN, GLOBAL_D), jnp.float32) * s, 'Wgv': jax.random.normal(ks[9], (D_IN, D_IN), jnp.float32) * s, 'bgv': jax.random.normal(ks[10], (D_IN,), jnp.float32) * 0.01, 'Wes': jax.random.normal(ks[11], (D_IN, 1), jnp.float32) * s, 'Wev': jax.random.normal(ks[12], (D_IN, D_IN), jnp.float32) * s, 'bev': jax.random.normal(ks[13], (D_IN,), jnp.float32) * 0.01}
    _L0_gnn_all = _L0_gnn_setup()
    _L0_gnn_in = {k: v for k, v in _L0_gnn_all.items() if k in ('masked_x', 'Wlq', 'Wlk', 'Wlv', 'blv', 'Wgq', 'Wgk', 'Wgv', 'bgv', 'Wes', 'Wev', 'bev')}
    del _L0_gnn_all
    return {'x': x, 'adj': adj, 'L0_gnn_masked_x': _L0_gnn_in['masked_x'], 'L0_gnn_Wlq': _L0_gnn_in['Wlq'], 'L0_gnn_Wlk': _L0_gnn_in['Wlk'], 'L0_gnn_Wlv': _L0_gnn_in['Wlv'], 'L0_gnn_blv': _L0_gnn_in['blv'], 'L0_gnn_Wgq': _L0_gnn_in['Wgq'], 'L0_gnn_Wgk': _L0_gnn_in['Wgk'], 'L0_gnn_Wgv': _L0_gnn_in['Wgv'], 'L0_gnn_bgv': _L0_gnn_in['bgv'], 'L0_gnn_Wes': _L0_gnn_in['Wes'], 'L0_gnn_Wev': _L0_gnn_in['Wev'], 'L0_gnn_bev': _L0_gnn_in['bev']}

def reference(x, adj, L0_gnn_masked_x, L0_gnn_Wlq, L0_gnn_Wlk, L0_gnn_Wlv, L0_gnn_blv, L0_gnn_Wgq, L0_gnn_Wgk, L0_gnn_Wgv, L0_gnn_bgv, L0_gnn_Wes, L0_gnn_Wev, L0_gnn_bev):
    import jax
    import jax.numpy as jnp

    def _L0_gnn_ref(adj_matrix, x, masked_x, Wlq, Wlk, Wlv, blv, Wgq, Wgk, Wgv, bgv, Wes, Wev, bev):
        import jax, jax.numpy as jnp
        import numpy as np
        import math
        N = 4096
        D_IN = 256
        LOCAL_D = 256
        GLOBAL_D = 256
        scale = 1.0 / math.sqrt(D_IN)
        x_bar = jnp.mean(x, axis=0, keepdims=True)
        lQ = masked_x @ Wlq
        lK = x @ Wlk
        lV = x @ Wlv + blv
        gQ = masked_x @ Wgq
        gK = x_bar @ Wgk
        gV = x_bar @ Wgv + bgv
        es = masked_x @ Wes
        eV = masked_x @ Wev + bev
        local_scores = lQ @ lK.T * scale
        local_scores = jnp.where(adj_matrix, local_scores, jnp.float32(-1000000000.0))
        global_scores = gQ @ gK.T * scale
        max_score = jnp.maximum(jnp.max(local_scores, axis=1, keepdims=True), jnp.maximum(global_scores, es))
        le = jnp.exp(local_scores - max_score)
        ge = jnp.exp(global_scores - max_score)
        ee = jnp.exp(es - max_score)
        denom = jnp.sum(le, axis=-1, keepdims=True) + ge + ee
        res = le / denom @ lV + ge / denom * gV + ee / denom * eV
        x_recon = jnp.maximum(res, masked_x)
        return x_recon
    x = _layernorm(x + _L0_gnn_ref(adj, x, L0_gnn_masked_x, L0_gnn_Wlq, L0_gnn_Wlk, L0_gnn_Wlv, L0_gnn_blv, L0_gnn_Wgq, L0_gnn_Wgk, L0_gnn_Wgv, L0_gnn_bgv, L0_gnn_Wes, L0_gnn_Wev, L0_gnn_bev), axis=-1)
    return x

_drawn_inputs = setup_inputs


def setup_inputs(seed=0):
    import zlib

    import numpy as np

    out = dict(_drawn_inputs(seed))
    spreads = {}
    factors = {'L0_gnn_blv': 8.0,
     'L0_gnn_Wgq': 64.0,
     'L0_gnn_Wgk': 64.0,
     'L0_gnn_Wgv': 64.0,
     'L0_gnn_bgv': 64.0,
     'L0_gnn_Wes': 2.816,
     'L0_gnn_bev': 41.158}
    for name, (base, spread) in spreads.items():
        noise = np.random.default_rng([zlib.crc32(name.encode()), seed]).standard_normal(out[name].shape)
        drawn = base * np.exp(spread * noise) if base else spread * noise
        out[name] = jnp.asarray(drawn.astype(out[name].dtype))
    for name, factor in factors.items():
        out[name] = (out[name] * factor).astype(out[name].dtype)
    return out
```

```python
from contextlib import ExitStack

import concourse.bass as bass
from concourse import mybir
from concourse.alu_op_type import AluOpType as ALU

F32 = mybir.dt.float32
F32R = mybir.dt.float32r
U8 = mybir.dt.uint8
ACT = mybir.ActivationFunctionType
AX_X = mybir.AxisListType.X

P = 128
N = 4096
D = 256
C = D // P
TILES = N // P
PAIRS = TILES // 2
KEYS = 512
BLOCKS = N // KEYS
SUB = KEYS // P
PIECES = 4
PIECE = N // PIECES
SCALE = D ** -0.5
MASKED = 1.0e9
LOWEST = -3.0e38
EPS = 1.0e-5

S_BANK, T_BANK, O_BANK, Q_BANK, E_BANK = 0, 2, 4, 6, 7


def back(i, par, n):
    return i - (n + 1 - par) // 2, (par - n) % 2


def exists(i):
    return not isinstance(i, int) or 0 <= i < PAIRS


def at_least(engine, semaphore, value):
    if not isinstance(value, int) or value > 0:
        engine.wait_ge(semaphore, value)


def keep_apart(engine):
    engine.nop(nofuse=True)


def gnn_resnorm(nc, x, adj, masked_x, wlq, wlk, wlv, blv, wgq, wgk, wgv, bgv, wes, wev, bev, out):
    with ExitStack() as ctx:
        def sb(name, shape, dt, where=ctx):
            return where.enter_context(nc.sbuf_tensor(name, shape, dt))

        def sem(name):
            return ctx.enter_context(nc.semaphore(name))

        xt_hi = sb("xt_hi", [P, C, N], F32R)
        xt_lo = sb("xt_lo", [P, C, N], F32R)
        val = sb("val", [P, N // P, 2 * D], F32R)
        ident = sb("ident", [P, P], F32)
        a_hi = sb("a_hi", [P, C, D], F32R)
        a_lo = sb("a_lo", [P, C, D], F32R)
        we_hi = sb("we_hi", [P, C, D + 2], F32R)
        we_lo = sb("we_lo", [P, C, D + 2], F32R)
        bias_pick = sb("bias_pick", [P, P], F32R)
        bias_e = sb("bias_e", [P, D + 2], F32R)
        gv = sb("gv", [P, D], F32)
        minus_half = sb("minus_half", [P, 1], F32)
        adj_in = [sb("adj_in0", [P, N], U8)]
        m_in = sb("m_in", [P, 2, D], F32)
        mt_hi = sb("mt_hi", [P, C, 2 * P], F32R)
        mt_lo = sb("mt_lo", [P, C, 2 * P], F32R)
        qt_hi = [sb(f"qt_hi{k}", [P, C, P], F32R) for k in range(2)]
        qt_lo = [sb(f"qt_lo{k}", [P, C, P], F32R) for k in range(2)]

        prep = ExitStack()
        raw = {k: sb(f"raw_{k}", [P, C, D], F32, prep) for k in ("wlq", "wlk", "wgq", "wgk", "wgv")}
        wq_t = sb("wq_t", [P, C, D], F32, prep)
        wk_t = sb("wk_t", [P, C, D], F32, prep)
        x_in = [sb(f"x_in{k}", [P, SUB, D], F32, prep) for k in range(2)]
        xs_hi = [sb(f"xs_hi{k}", [P, C, KEYS], F32R, prep) for k in range(2)]
        xs_lo = [sb(f"xs_lo{k}", [P, C, KEYS], F32R, prep) for k in range(2)]
        raw["wlv"] = sb("raw_wlv", [P, C, D], F32, prep)
        raw["we"] = sb("raw_we", [P, C, D + 2], F32, prep)
        wv_hi = sb("wv_hi", [P, C, D], F32R, prep)
        wv_lo = sb("wv_lo", [P, C, D], F32R, prep)
        raw_bias = sb("raw_bias", [P, 2, D], F32, prep)
        low_bias = sb("low_bias", [P, 2, D], F32R, prep)
        bias_v = sb("bias_v", [P, D], F32R, prep)
        bgv_all = sb("bgv_all", [P, D], F32, prep)
        xsum = sb("xsum", [P, C, BLOCKS], F32, prep)
        xtot = sb("xtot", [P, C], F32, prep)
        xmean = sb("xmean", [P, C, P], F32, prep)
        gk = sb("gk", [P, C], F32, prep)
        prep.close()
        score = [sb(f"score{k}", [P, N], F32) for k in range(2)]
        adj_in.append(sb("adj_in1", [P, N], U8))
        pt_hi = [sb(f"pt_hi{k}", [P, KEYS], F32R) for k in range(2)]
        pt_lo = [sb(f"pt_lo{k}", [P, KEYS], F32R) for k in range(2)]
        fin_in = [sb(f"fin_in{k}", [P, 2, D], F32) for k in range(2)]
        ev = [sb(f"ev{k}", [P, D + 2 + BLOCKS], F32) for k in range(2)]
        neg_max = [sb(f"neg_max{k}", [P, 1], F32) for k in range(2)]
        parts = [sb(f"parts{k}", [P, PIECES + 2], F32) for k in range(2)]
        den = sb("den", [P, 1], F32)
        rden = sb("rden", [P, 1], F32)
        acc = sb("acc", [P, D], F32)
        stats = sb("stats", [P, 6], F32)
        mean_var = sb("mean_var", [P, 2], F32)
        var_eps = sb("var_eps", [P, 1], F32)
        rstd = sb("rstd", [P, 1], F32)
        y = [sb(f"y{k}", [P, D], F32) for k in range(2)]

        ps = ctx.enter_context(nc.psum_tensor("ps", [P, 8, KEYS], F32))

        consts_ready = sem("consts_ready")
        wl_loaded = sem("wl_loaded")
        wv_loaded = sem("wv_loaded")
        wg_loaded = sem("wg_loaded")
        x_loaded = [sem(f"x_loaded{k}") for k in range(2)]
        prep_pe = sem("prep_pe")
        prep_dve = sem("prep_dve")
        xt_ready = sem("xt_ready")
        xs_hi_ready = sem("xs_hi_ready")
        xs_ready = sem("xs_ready")
        v_ready = sem("v_ready")
        v_hi_ready = sem("v_hi_ready")
        v_split = sem("v_split")
        x_stored = sem("x_stored")
        adj_loaded = [sem(f"adj_loaded{k}") for k in range(2)]
        m_loaded = sem("m_loaded")
        fin_loaded = [sem(f"fin_loaded{k}") for k in range(2)]
        out_stored = [sem(f"out_stored{k}") for k in range(2)]
        bias_ready = sem("bias_ready")
        s_ready = sem("s_ready")
        s_masked = sem("s_masked")
        max_ready = sem("max_ready")
        exp_ready = sem("exp_ready")
        ge_ready = sem("ge_ready")
        t_ready = sem("t_ready")
        pt_hi_ready = sem("pt_hi_ready")
        pt_ready = sem("pt_ready")
        pv_done = sem("pv_done")
        mt_ready = sem("mt_ready")
        mt_hi_ready = sem("mt_hi_ready")
        mt_split = sem("mt_split")
        q_ready = sem("q_ready")
        qt_hi_ready = sem("qt_hi_ready")
        qt_split = sem("qt_split")
        e_ready = sem("e_ready")
        e_copied = sem("e_copied")
        den_ready = sem("den_ready")
        rden_ready = sem("rden_ready")
        gv_added = sem("gv_added")
        o_used = sem("o_used")
        ev_used = sem("ev_used")
        res_ready = sem("res_ready")
        fin_used = sem("fin_used")
        stats_ready = sem("stats_ready")
        mean_ready = sem("mean_ready")
        y_ready = sem("y_ready")
        var_ready = sem("var_ready")
        rstd_ready = sem("rstd_ready")

        block = ctx.enter_context(nc.Block())

        x_blocks = x.rearrange("(b a p) d -> b p a d", a=SUB, p=P)
        m_pairs = masked_x.rearrange("(i a p) d -> i p a d", a=2, p=P)
        m_tiles = masked_x.rearrange("(t p) d -> t p d", p=P)
        x_tiles = x.rearrange("(t p) d -> t p d", p=P)
        adj_tiles = adj.rearrange("(t p) n -> t p n", p=P)
        out_tiles = out.rearrange("(t p) d -> t p d", p=P)

        def rows_by_chunk(w):
            return w.rearrange("(r p) n -> p r n", p=P)

        def one_row(b):
            return b.rearrange("(a n) -> a n", a=1)

        @block.sync
        def _(sp):
            def load_x(b, par, i):
                sp.dma_start(x_in[par][:], x_blocks[b]).then_inc(x_loaded[par], 16)

            sp.dma_start(raw["wlq"][:], rows_by_chunk(wlq)).then_inc(wl_loaded, 16)
            sp.dma_start(raw["wlk"][:], rows_by_chunk(wlk)).then_inc(wl_loaded, 16)
            sp.dma_start(m_in[:], m_pairs[0]).then_inc(m_loaded, 16)
            load_x(0, 0, 0)
            sp.dma_start(raw["wlv"][:], rows_by_chunk(wlv)).then_inc(wv_loaded, 16)
            sp.wait_ge(consts_ready, 1)
            for row in (0, 32):
                sp.dma_start(raw_bias[row:row + 1, 0, :], one_row(blv)).then_inc(wv_loaded, 16)
                sp.dma_start(raw_bias[row:row + 1, 1, :], one_row(bev)).then_inc(wv_loaded, 16)
            load_x(1, 1, 0)
            for name, w in (("wgq", wgq), ("wgk", wgk), ("wgv", wgv)):
                sp.dma_start(raw[name][:], rows_by_chunk(w)).then_inc(wg_loaded, 16)
            sp.dma_start(raw["we"][:, :, 0:D], rows_by_chunk(wev)).then_inc(wg_loaded, 16)
            with nc.allow_non_contiguous_dma(reason="one column"):
                sp.dma_start(raw["we"][:, :, D + 1:D + 2], rows_by_chunk(wes)).then_inc(wg_loaded, 16)
            sp.dma_start(bgv_all[:], one_row(bgv).to_broadcast([P, D])).then_inc(wg_loaded, 16)
            with sp.Fori(0, BLOCKS // 2 - 1) as i:
                for par in range(2):
                    sp.wait_ge(xt_ready, 2 * i + par + 1)
                    load_x(2 * i + par + 2, par, i)
            sp.dma_start(adj_in[0][:], adj_tiles[0]).then_inc(adj_loaded[0], 16)
            sp.wait_ge(prep_pe, PREP_PE)
            sp.wait_ge(prep_dve, PREP_DVE)
            sp.dma_start(adj_in[1][:], adj_tiles[1]).then_inc(adj_loaded[1], 16)

            def tile(i, par):
                t = 2 * i + par
                if exists(i + 1):
                    at_least(sp, bias_ready, PIECES * (t + 1))
                    sp.dma_start(adj_in[par][:], adj_tiles[t + 2]).then_inc(adj_loaded[par], 16)
                    if par == 0:
                        sp.wait_ge(mt_ready, i + 1)
                        sp.dma_start(m_in[:], m_pairs[i + 1]).then_inc(m_loaded, 16)
                if exists(i):
                    at_least(sp, fin_used, t - 1)
                    sp.dma_start(fin_in[par][:, 0, :], m_tiles[t]).then_inc(fin_loaded[par], 16)
                    sp.dma_start(fin_in[par][:, 1, :], x_tiles[t]).then_inc(fin_loaded[par], 16)
                if exists(i - 1):
                    sp.wait_ge(y_ready, t - 1)
                    sp.dma_start(out_tiles[t - 2], y[par][:]).then_inc(out_stored[par], 16)

            for i in range(1):
                tile(i, 0)
                tile(i, 1)
            with sp.Fori(1, PAIRS - 1) as i:
                tile(i, 0)
                tile(i, 1)
            for i in (PAIRS - 1, PAIRS):
                tile(i, 0)
                tile(i, 1)
            for par in range(2):
                sp.wait_ge(out_stored[par], 16 * PAIRS)

        @block.gpsimd
        def _(gp):
            gp.memset(raw_bias[:], 0.0).then_inc(consts_ready, 1)
            gp.memset(ident[:], 0.0).then_inc(consts_ready, 1)
            gp.wait_ge(consts_ready, 2)
            gp.affine_select(out=ident[:], in_=ident[:], compare_op=ALU.not_equal, fill=1.0, base=0,
                             pattern=[[-1, P]], channel_multiplier=1).then_inc(consts_ready, 1)
            gp.memset(bias_pick[:].bitcast(F32), 0.0).then_inc(consts_ready, 1)
            gp.memset(bias_v[:].bitcast(F32), 0.0).then_inc(consts_ready, 1)
            gp.memset(bias_e[:].bitcast(F32), 0.0).then_inc(consts_ready, 1)
            gp.memset(minus_half[:], -0.5).then_inc(consts_ready, 1)
            gp.wait_ge(consts_ready, 7)
            for row in (0, 32):
                gp.memset(bias_pick[row:row + 1, :].bitcast(F32), 1.0).then_inc(consts_ready, 1)

            def bias(i, par, piece):
                t = 2 * i + par
                if piece == 0:
                    gp.wait_ge(adj_loaded[par], 16 * (i + 1))
                cols = slice(piece * PIECE, (piece + 1) * PIECE)
                if not isinstance(i, int) or i > 0:
                    gp.wait_ge(t_ready, BLOCKS * (t - 2) + (piece + 1) * BLOCKS // PIECES)
                elif piece == 0 and par == 0:
                    gp.wait_ge(prep_dve, PREP_DVE)
                    gp.wait_ge(prep_pe, PREP_PE)
                keep_apart(gp)
                gp.tensor_scalar(score[par][:, cols], adj_in[par][:, cols], -1.0, MASKED,
                                 ALU.add, ALU.mult).then_inc(bias_ready, 1)

            def inverse_deviation(i, par):
                t = 2 * i + par
                gp.wait_ge(mean_ready, t + 1)
                keep_apart(gp)
                gp.tensor_scalar(var_eps[:], mean_var[:, 1:2], EPS, 1.0, ALU.add,
                                 ALU.mult).then_inc(var_ready, 1)
                gp.wait_ge(var_ready, t + 1)
                gp.tensor_tensor(rstd[:], var_eps[:], minus_half[:], ALU.pow).then_inc(rstd_ready, 1)

            def tile(i, par):
                ni, npar = back(i, par, -1)
                fi, fpar = back(i, par, 2)
                if exists(ni):
                    bias(ni, npar, 0)
                    bias(ni, npar, 1)
                if exists(fi):
                    inverse_deviation(fi, fpar)
                if exists(ni):
                    bias(ni, npar, 2)
                    bias(ni, npar, 3)

            for piece in range(PIECES):
                bias(0, 0, piece)
            tile(0, 0)
            tile(0, 1)
            with gp.Fori(1, PAIRS - 1) as i:
                tile(i, 0)
                tile(i, 1)
            for i in (PAIRS - 1, PAIRS):
                tile(i, 0)
                tile(i, 1)

        @block.tensor
        def _(pe):
            def three_passes(o, w_hi, w_lo, m_hi, m_lo, start, stop):
                pe.matmul(o, w_hi, m_hi, start=start, stop=False, skip_group_check=True)
                pe.matmul(o, w_hi, m_lo, start=False, stop=False, skip_group_check=True)
                return pe.matmul(o, w_lo, m_hi, start=False, stop=stop, skip_group_check=True)

            def transpose_weight(w, bank):
                for cc in range(C):
                    for r in range(C):
                        last = pe.transpose(ps[:, bank, cc * D + r * P:cc * D + (r + 1) * P],
                                            w[:, r, cc * P:(cc + 1) * P], ident[:])
                return last

            def transpose_masked_x(i):
                pe.wait_ge(m_loaded, 16 * (i + 1))
                if not isinstance(i, int) or i > 0:
                    pe.wait_ge(e_copied, 2 * i)
                for cc in range(C):
                    for a in range(2):
                        last = pe.transpose(ps[:, E_BANK, cc * D + a * P:cc * D + (a + 1) * P],
                                            m_in[:, a, cc * P:(cc + 1) * P], ident[:])
                last.then_inc(mt_ready, 1)

            def queries(i):
                pe.wait_ge(mt_split, i + 1)
                if not isinstance(i, int) or i > 0:
                    pe.wait_ge(qt_split, 2 * i)
                for oc in range(C):
                    for cc in range(C):
                        cols = slice(oc * P, (oc + 1) * P)
                        last = three_passes(ps[:, Q_BANK, oc * D:(oc + 1) * D], a_hi[:, cc, cols],
                                            a_lo[:, cc, cols], mt_hi[:, cc, :], mt_lo[:, cc, :],
                                            cc == 0, cc == C - 1)
                last.then_inc(q_ready, 1)

            pe.wait_ge(consts_ready, 9)
            pe.wait_ge(wl_loaded, 32)
            transpose_weight(raw["wlq"], 0)
            transpose_weight(raw["wlk"], 1).then_inc(prep_pe, 1)
            transpose_masked_x(0)
            pe.wait_ge(prep_dve, DVE_WT)
            for r in range(C):
                for cc in range(C):
                    last = pe.matmul(ps[:, 2, r * D:(r + 1) * D], wq_t[:, cc, r * P:(r + 1) * P],
                                     wk_t[:, cc, :], start=(cc == 0), stop=(cc == C - 1))
            last.then_inc(prep_pe, 1)
            pe.wait_ge(prep_dve, DVE_A)
            queries(0)

            def x_transpose(b, par, i):
                pe.wait_ge(x_loaded[par], 16 * (i + 1))
                at_least(pe, xs_ready, b - 1)
                for cc in range(C):
                    for a in range(SUB):
                        last = pe.transpose(ps[:, 2 * par + cc, a * P:(a + 1) * P],
                                            x_in[par][:, a, cc * P:(cc + 1) * P], ident[:])
                last.then_inc(xt_ready, 1)

            def values(b, par):
                pe.wait_ge(xs_ready, b + 1)
                pe.wait_ge(v_split, b)
                for a in range(SUB):
                    o = ps[:, O_BANK + 2 * par + a // 2, (a % 2) * D:(a % 2 + 1) * D]
                    rows = slice(a * P, (a + 1) * P)
                    for cc in range(C):
                        three_passes(o, xs_hi[par][:, cc, rows], xs_lo[par][:, cc, rows],
                                     wv_hi[:, cc, :], wv_lo[:, cc, :], cc == 0, False)
                    last = pe.matmul(o, bias_pick[:], bias_v[:], start=False, stop=True,
                                     skip_group_check=True)
                last.then_inc(v_ready, 1)

            pe.wait_ge(prep_dve, DVE_WV)
            pe.wait_ge(qt_split, 2)
            x_transpose(0, 0, 0)
            with pe.Fori(0, BLOCKS // 2 - 1) as i:
                x_transpose(2 * i + 1, 1, i)
                values(2 * i, 0)
                x_transpose(2 * i + 2, 0, i + 1)
                values(2 * i + 1, 1)
            x_transpose(BLOCKS - 1, 1, BLOCKS // 2 - 1)
            values(BLOCKS - 2, 0)
            values(BLOCKS - 1, 1)

            pe.wait_ge(wg_loaded, 16 * 6)
            pe.wait_ge(v_split, BLOCKS + 1)
            transpose_weight(raw["wgq"], 2).then_inc(prep_pe, 1)
            pe.wait_ge(prep_dve, DVE_MEAN)
            for oc in range(C):
                for cc in range(C):
                    pe.matmul(ps[:, 4, oc:oc + 1], raw["wgk"][:, cc, oc * P:(oc + 1) * P],
                              xmean[:, cc, 0:1], start=(cc == 0), stop=(cc == C - 1))
            for cc in range(C):
                last = pe.matmul(ps[:, 5, 0:D], xmean[:, cc, :], raw["wgv"][:, cc, :],
                                 start=(cc == 0), stop=(cc == C - 1))
            last.then_inc(prep_pe, 1)
            pe.wait_ge(prep_dve, DVE_GK)
            for oc in range(C):
                for cc in range(C):
                    last = pe.matmul(ps[:, 6, oc:oc + 1], wq_t[:, cc, oc * P:(oc + 1) * P],
                                     gk[:, cc:cc + 1], start=(cc == 0), stop=(cc == C - 1))
            last.then_inc(prep_pe, 1)
            pe.wait_ge(prep_dve, PREP_DVE)

            def scores(i, par, j):
                s = 2 * BLOCKS * i + BLOCKS * par + j
                if j == 0:
                    pe.wait_ge(qt_split, 2 * i + par + 1)
                at_least(pe, s_masked, s - 1)
                for cc in range(C):
                    keys = slice(j * KEYS, (j + 1) * KEYS)
                    last = three_passes(ps[:, S_BANK + j % 2, :], qt_hi[par][:, cc, :],
                                        qt_lo[par][:, cc, :], xt_hi[:, cc, keys],
                                        xt_lo[:, cc, keys], cc == 0, cc == C - 1)
                last.then_inc(s_ready, 1)

            def transpose_weights(i, par, g):
                u = 2 * BLOCKS * i + BLOCKS * par + g
                if g % 2 == 0:
                    pe.wait_ge(exp_ready, PIECES * (2 * i + par) + g * PIECES // BLOCKS + 1)
                at_least(pe, pt_ready, u - 1)
                for k in range(SUB):
                    last = pe.transpose(ps[:, T_BANK + g % 2, k * P:(k + 1) * P],
                                        score[par][:, g * KEYS + k * P:g * KEYS + (k + 1) * P],
                                        ident[:])
                last.then_inc(t_ready, 1)

            def weigh_values(i, par, g):
                u = 2 * BLOCKS * i + BLOCKS * par + g
                pe.wait_ge(pt_ready, u + 1)
                if g == 0:
                    at_least(pe, o_used, 2 * i + par - 1)
                for k in range(SUB):
                    chunk = g * SUB + k
                    w = slice(k * P, (k + 1) * P)
                    pe.matmul(ps[:, O_BANK + par, :], pt_hi[g % 2][:, w], val[:, chunk, :],
                              start=(chunk == 0), stop=False, skip_group_check=True)
                    last = pe.matmul(ps[:, O_BANK + par, 0:D], pt_lo[g % 2][:, w], val[:, chunk, 0:D],
                                     start=False, stop=(chunk == N // P - 1), skip_group_check=True)
                last.then_inc(pv_done, 1)

            def self_values(i, par):
                pe.wait_ge(mt_split, i + 1)
                at_least(pe, e_copied, 2 * i + par)
                rows = slice(par * P, (par + 1) * P)
                o = ps[:, E_BANK, 0:D + 2]
                for cc in range(C):
                    three_passes(o, mt_hi[:, cc, rows], mt_lo[:, cc, rows], we_hi[:, cc, :],
                                 we_lo[:, cc, :], cc == 0, False)
                pe.matmul(o, bias_pick[:], bias_e[:], start=False, stop=True,
                          skip_group_check=True).then_inc(e_ready, 1)

            def slot(i, par, j):
                if exists(i):
                    scores(i, par, j)
                ti, tpar = back(i, par, 1 if j >= 1 else 2)
                if exists(ti):
                    transpose_weights(ti, tpar, (j - 1) % BLOCKS)
                vi, vpar = back(i, par, 1 if j >= 2 else 2)
                if exists(vi):
                    weigh_values(vi, vpar, (j - 2) % BLOCKS)
                if j == 4 and exists(i):
                    self_values(i, par)
                if par == 1 and exists(i) and exists(i + 1):
                    if j == 5:
                        transpose_masked_x(i + 1)
                    if j == 6:
                        queries(i + 1)

            def pair(i):
                for par in range(2):
                    for j in range(BLOCKS):
                        slot(i, par, j)

            pair(0)
            with pe.Fori(1, PAIRS - 1) as i:
                pair(i)
            pair(PAIRS - 1)
            pair(PAIRS)

        @block.scalar
        def _(act):
            def x_hi(b, par):
                act.wait_ge(xt_ready, b + 1)
                at_least(act, v_ready, b - 1)
                for cc in range(C):
                    act.activation(xs_hi[par][:, cc, :], ps[:, 2 * par + cc, :], ACT.Copy,
                                   accum_out=xsum[:, cc, bass.ds(b, 1)])
                act.activation(xt_hi[:, :, bass.ds(b * KEYS, KEYS)], ps[:, 2 * par:2 * par + 2, :],
                               ACT.Copy).then_inc(xs_hi_ready, 1)

            def v_hi(b, par):
                act.wait_ge(v_ready, b + 1)
                act.activation(val[:, bass.ds(b * SUB, SUB), 0:D],
                               ps[:, O_BANK + 2 * par:O_BANK + 2 * par + 2, :].rearrange(
                                   "p b (a n) -> p (b a) n", a=2),
                               ACT.Copy).then_inc(v_hi_ready, 1)

            act.wait_ge(consts_ready, 9)
            x_hi(0, 0)
            with act.Fori(0, BLOCKS // 2 - 1) as i:
                x_hi(2 * i + 1, 1)
                v_hi(2 * i, 0)
                x_hi(2 * i + 2, 0)
                v_hi(2 * i + 1, 1)
            x_hi(BLOCKS - 1, 1)
            v_hi(BLOCKS - 2, 0)
            v_hi(BLOCKS - 1, 1)

            def exps(i, par, piece):
                t = 2 * i + par
                if piece == 0:
                    act.wait_ge(max_ready, t + 1)
                    at_least(act, ev_used, t - 1)
                    act.activation(parts[par][:, PIECES:PIECES + 2], ev[par][:, D:D + 2], ACT.Exp,
                                   bias=neg_max[par][:]).then_inc(ge_ready, 1)
                cols = slice(piece * PIECE, (piece + 1) * PIECE)
                act.activation(score[par][:, cols], score[par][:, cols], ACT.Exp,
                               bias=neg_max[par][:],
                               accum_out=parts[par][:, piece:piece + 1]).then_inc(exp_ready, 1)

            def weights_hi(i, par, g):
                u = 2 * BLOCKS * i + BLOCKS * par + g
                act.wait_ge(t_ready, u + 1)
                at_least(act, pv_done, u - 1)
                act.activation(pt_hi[g % 2][:], ps[:, T_BANK + g % 2, :],
                               ACT.Copy).then_inc(pt_hi_ready, 1)

            def copy_self_values(i, par):
                t = 2 * i + par
                act.wait_ge(e_ready, t + 1)
                at_least(act, ev_used, t - 1)
                act.activation(ev[par][:, 0:D + 2], ps[:, E_BANK, 0:D + 2],
                               ACT.Copy).then_inc(e_copied, 1)

            def slot(i, par, j):
                pi, ppar = back(i, par, 1)
                if j < PIECES and exists(pi):
                    exps(pi, ppar, j)
                ti, tpar = back(i, par, 1 if j >= 1 else 2)
                if exists(ti):
                    weights_hi(ti, tpar, (j - 1) % BLOCKS)
                if j == 4 and exists(i):
                    copy_self_values(i, par)

            def pair(i):
                for par in range(2):
                    for j in range(BLOCKS):
                        slot(i, par, j)

            act.wait_ge(prep_dve, PREP_DVE)
            pair(0)
            with act.Fori(1, PAIRS - 1) as i:
                pair(i)
            pair(PAIRS - 1)
            pair(PAIRS)

        @block.vector
        def _(dve):
            def split_masked_x(i):
                both = ps[:, E_BANK, :].rearrange("p (c n) -> p c n", c=C)
                dve.wait_ge(mt_ready, i + 1)
                if not isinstance(i, int) or i > 0:
                    dve.wait_ge(e_ready, 2 * i)
                dve.tensor_copy(mt_hi[:], both).then_inc(mt_hi_ready, 1)
                dve.wait_ge(mt_hi_ready, i + 1)
                dve.tensor_tensor(mt_lo[:], both, mt_hi[:].bitcast(F32),
                                  ALU.subtract).then_inc(mt_split, 1)

            def split_queries(i, par):
                t = 2 * i + par
                mine = ps[:, Q_BANK, :].rearrange("p (c n) -> p c n", c=C)[:, :, par * P:(par + 1) * P]
                dve.wait_ge(q_ready, i + 1)
                if not isinstance(i, int) or i > 0:
                    dve.wait_ge(s_ready, BLOCKS * (t - 1))
                dve.tensor_copy(qt_hi[par][:], mine).then_inc(qt_hi_ready, 1)
                dve.wait_ge(qt_hi_ready, t + 1)
                dve.tensor_tensor(qt_lo[par][:], mine, qt_hi[par][:].bitcast(F32),
                                  ALU.subtract).then_inc(qt_split, 1)

            steps = [0]

            def step(ins):
                steps[0] += 1
                ins.then_inc(prep_dve, 1)
                dve.wait_ge(prep_dve, steps[0])

            def at(mark):
                assert steps[0] == mark, (steps[0], mark)

            two = "p (c n) -> p c n"
            dve.wait_ge(prep_pe, 1)
            step(dve.tensor_copy(wq_t[:], ps[:, 0, :].rearrange(two, c=C)))
            step(dve.tensor_copy(wk_t[:], ps[:, 1, :].rearrange(two, c=C)))
            at(DVE_WT)
            split_masked_x(0)
            dve.wait_ge(prep_pe, 2)
            a_psum = ps[:, 2, :].rearrange(two, c=C)
            step(dve.tensor_scalar(a_hi[:], a_psum, SCALE, None, ALU.mult))
            step(dve.scalar_tensor_tensor(a_lo[:], a_psum, SCALE, a_hi[:].bitcast(F32), ALU.mult,
                                          ALU.subtract))
            at(DVE_A)
            dve.wait_ge(wv_loaded, 16 * 5)
            step(dve.tensor_copy(wv_hi[:], raw["wlv"][:]))
            step(dve.tensor_tensor(wv_lo[:], raw["wlv"][:], wv_hi[:].bitcast(F32), ALU.subtract))
            dve.wait_ge(consts_ready, 9)
            step(dve.tensor_copy(low_bias[32:33, :, :], raw_bias[32:33, :, :]))
            for n, b in ((0, bias_v), (1, bias_e)):
                step(dve.tensor_copy(b[0:1, 0:D], raw_bias[0:1, n, :]))
                step(dve.tensor_tensor(b[32:33, 0:D], raw_bias[32:33, n, :],
                                       low_bias[32:33, n, :].bitcast(F32), ALU.subtract))
            at(DVE_WV)
            split_queries(0, 0)
            split_queries(0, 1)
            dve.memset(gk[:], 0.0).then_inc(v_split, 1)

            def x_lo(b, par):
                dve.wait_ge(xs_hi_ready, b + 1)
                at_least(dve, x_stored, b - 1)
                dve.tensor_tensor(xs_lo[par][:], ps[:, 2 * par:2 * par + 2, :],
                                  xs_hi[par][:].bitcast(F32), ALU.subtract).then_inc(xs_ready, 1)

            def x_store(b, par):
                dve.wait_ge(xs_ready, b + 1)
                dve.tensor_copy(xt_lo[:, :, bass.ds(b * KEYS, KEYS)],
                                xs_lo[par][:].bitcast(F32)).then_inc(x_stored, 1)

            def v_lo(b, par):
                dve.wait_ge(v_hi_ready, b + 1)
                chunks = bass.ds(b * SUB, SUB)
                dve.tensor_tensor(val[:, chunks, D:2 * D],
                                  ps[:, O_BANK + 2 * par:O_BANK + 2 * par + 2, :].rearrange(
                                      "p b (a n) -> p (b a) n", a=2),
                                  val[:, chunks, 0:D].bitcast(F32), ALU.subtract).then_inc(v_split, 1)

            x_lo(0, 0)
            x_store(0, 0)
            with dve.Fori(0, BLOCKS // 2 - 1) as i:
                x_lo(2 * i + 1, 1)
                x_store(2 * i + 1, 1)
                v_lo(2 * i, 0)
                x_lo(2 * i + 2, 0)
                x_store(2 * i + 2, 0)
                v_lo(2 * i + 1, 1)
            x_lo(BLOCKS - 1, 1)
            x_store(BLOCKS - 1, 1)
            v_lo(BLOCKS - 2, 0)
            v_lo(BLOCKS - 1, 1)

            step(dve.tensor_reduce(xtot[:], xsum[:], AX_X, ALU.add))
            for cc in range(C):
                step(dve.tensor_scalar(xmean[:, cc, :], xtot[:, cc:cc + 1].to_broadcast([P, P]),
                                       1.0 / N, None, ALU.mult))
            at(DVE_MEAN)
            dve.wait_ge(prep_pe, 3)
            step(dve.tensor_copy(wq_t[:], ps[:, 2, :].rearrange(two, c=C)))
            dve.wait_ge(prep_pe, 4)
            step(dve.tensor_copy(gk[:], ps[:, 4, 0:C]))
            at(DVE_GK)
            step(dve.tensor_tensor(gv[:], ps[:, 5, 0:D], bgv_all[:], ALU.add))
            for cc in range(C):
                dve.wait_ge(wg_loaded, 16 * 6)
            dve.wait_ge(prep_pe, 5)
            step(dve.tensor_scalar(raw["we"][:, :, D:D + 1], ps[:, 6, 0:C].rearrange(
                "p (c n) -> p c n", n=1), SCALE, None, ALU.mult))
            step(dve.tensor_copy(we_hi[:], raw["we"][:]))
            step(dve.tensor_tensor(we_lo[:], raw["we"][:], we_hi[:].bitcast(F32), ALU.subtract))
            at(PREP_DVE)

            def mask_scores(i, par, j):
                s = 2 * BLOCKS * i + BLOCKS * par + j
                dve.wait_ge(s_ready, s + 1)
                if j % 2 == 0:
                    dve.wait_ge(bias_ready, PIECES * (2 * i + par) + j * PIECES // BLOCKS + 1)
                keep_apart(dve)
                mine = score[par][:, j * KEYS:(j + 1) * KEYS]
                dve.tensor_tensor_reduce(mine, ps[:, S_BANK + j % 2, :], mine, 1.0, LOWEST, ALU.add,
                                         ALU.max, ev[par][:, D + 2 + j:D + 3 + j]).then_inc(s_masked, 1)

            def row_max(i, par):
                t = 2 * i + par
                dve.wait_ge(s_masked, BLOCKS * (t + 1))
                dve.wait_ge(e_copied, t + 1)
                dve.tensor_reduce(neg_max[par][:], ev[par][:, D:], AX_X, ALU.max,
                                  negate=True).then_inc(max_ready, 1)

            def weights_lo(i, par, g):
                u = 2 * BLOCKS * i + BLOCKS * par + g
                dve.wait_ge(pt_hi_ready, u + 1)
                dve.tensor_tensor(pt_lo[g % 2][:], ps[:, T_BANK + g % 2, :],
                                  pt_hi[g % 2][:].bitcast(F32), ALU.subtract).then_inc(pt_ready, 1)

            def finish(i, par, j):
                t = 2 * i + par
                o = ps[:, O_BANK + par, :]
                m_row, x_row = fin_in[par][:, 0, :], fin_in[par][:, 1, :]
                if j == 2:
                    dve.wait_ge(exp_ready, PIECES * (t + 1))
                    dve.tensor_reduce(den[:], parts[par][:], AX_X, ALU.add).then_inc(den_ready, 1)
                    dve.wait_ge(den_ready, t + 1)
                    dve.reciprocal(rden[:], den[:]).then_inc(rden_ready, 1)
                    dve.wait_ge(pv_done, BLOCKS * (t + 1))
                    dve.scalar_tensor_tensor(acc[:], gv[:], parts[par][:, PIECES:PIECES + 1],
                                             o[:, 0:D], ALU.mult, ALU.add).then_inc(gv_added, 1)
                    dve.wait_ge(gv_added, t + 1)
                    dve.tensor_tensor(acc[:], o[:, D:2 * D], acc[:], ALU.add).then_inc(o_used, 1)
                if j == 3:
                    dve.wait_ge(o_used, t + 1)
                    dve.scalar_tensor_tensor(acc[:], ev[par][:, 0:D], parts[par][:, PIECES + 1:PIECES + 2],
                                             acc[:], ALU.mult, ALU.add).then_inc(ev_used, 1)
                    dve.wait_ge(ev_used, t + 1)
                    dve.wait_ge(rden_ready, t + 1)
                    dve.wait_ge(fin_loaded[par], 32 * (i + 1))
                    dve.scalar_tensor_tensor(acc[:], acc[:], rden[:], m_row, ALU.mult,
                                             ALU.max).then_inc(res_ready, 1)
                    dve.wait_ge(res_ready, t + 1)
                    dve.tensor_tensor(acc[:], acc[:], x_row, ALU.add).then_inc(fin_used, 1)
                if j == 4:
                    dve.wait_ge(fin_used, t + 1)
                    dve.bn_stats(stats[:], acc[:]).then_inc(stats_ready, 1)
                    dve.wait_ge(stats_ready, t + 1)
                    keep_apart(dve)
                    dve.bn_aggr(mean_var[:], stats[:]).then_inc(mean_ready, 1)
                if j == 6:
                    dve.wait_ge(rstd_ready, t + 1)
                    at_least(dve, out_stored[par], 16 * i)
                    dve.tensor_scalar(y[par][:], acc[:], mean_var[:, 0:1], rstd[:], ALU.subtract,
                                      ALU.mult).then_inc(y_ready, 1)

            def slot(i, par, j):
                if par == 1 and exists(i) and exists(i + 1):
                    if j == 6:
                        split_masked_x(i + 1)
                    if j == 7:
                        split_queries(i + 1, 0)
                if par == 0 and exists(i) and j == 1 and not (isinstance(i, int) and i == 0):
                    split_queries(i, 1)
                if exists(i):
                    mask_scores(i, par, j)
                    if j == BLOCKS - 1:
                        row_max(i, par)
                ti, tpar = back(i, par, 1 if j >= 1 else 2)
                if exists(ti):
                    weights_lo(ti, tpar, (j - 1) % BLOCKS)
                fi, fpar = back(i, par, 2)
                if exists(fi):
                    finish(fi, fpar, j)

            def pair(i):
                for par in range(2):
                    for j in range(BLOCKS):
                        slot(i, par, j)

            pair(0)
            with dve.Fori(1, PAIRS - 1) as i:
                pair(i)
            pair(PAIRS - 1)
            pair(PAIRS)


DVE_WT = 2
DVE_A = 4
DVE_WV = 11
DVE_MEAN = 14
DVE_GK = 16
PREP_DVE = 20
PREP_PE = 5


_INS = ['x', 'adj', 'L0_gnn_masked_x', 'L0_gnn_Wlq', 'L0_gnn_Wlk', 'L0_gnn_Wlv', 'L0_gnn_blv',
        'L0_gnn_Wgq', 'L0_gnn_Wgk', 'L0_gnn_Wgv', 'L0_gnn_bgv', 'L0_gnn_Wes', 'L0_gnn_Wev', 'L0_gnn_bev']


def kernel(**inputs):
    import numpy as _np
    import concourse.bacc as _bacc
    from concourse import mybir as _mybir
    from concourse.bass_utils import run_bass_kernel_spmd as _run

    nc = _bacc.Bacc("TRN2", target_bir_lowering=False, num_devices=1)
    arrays, args = {}, []
    for name in _INS:
        a = _np.ascontiguousarray(inputs[name])
        arrays[f"in_{name}_dram"] = a
        args.append(nc.dram_tensor(f"in_{name}_dram", a.shape, _mybir.dt.from_np(a.dtype), kind="ExternalInput").ap())
    o = nc.dram_tensor("out_0_dram", (N, D), F32, kind="ExternalOutput").ap()
    gnn_resnorm(nc, *args, o)
    r = _run(nc, [arrays], core_ids=[0])
    return r.results[0]["out_0_dram"]
```

```python
from contextlib import ExitStack

import concourse.bass as bass
from concourse import mybir
from concourse.alu_op_type import AluOpType as ALU

F32 = mybir.dt.float32
F32R = mybir.dt.float32r
U8 = mybir.dt.uint8
ACT = mybir.ActivationFunctionType
AX_X = mybir.AxisListType.X

P = 128
N = 4096
D = 256
C = D // P
TILES = N // P
PAIRS = TILES // 2
KEYS = 512
BLOCKS = N // KEYS
SUB = KEYS // P
PIECES = 4
PIECE = N // PIECES
SCALE = D ** -0.5
MASKED = 1.0e9
LOWEST = -3.0e38
EPS = 1.0e-5

S_BANK, T_BANK, O_BANK, M_BANK, E_BANK = 0, 2, 4, 6, 7


def back(i, par, n):
    return i - (n + 1 - par) // 2, (par - n) % 2


def exists(i):
    return not isinstance(i, int) or 0 <= i < PAIRS


def at_least(engine, semaphore, value):
    if not isinstance(value, int) or value > 0:
        engine.wait_ge(semaphore, value)


def keep_apart(engine):
    engine.nop(nofuse=True)


def gnn_resnorm(nc, x, adj, masked_x, wlq, wlk, wlv, blv, wgq, wgk, wgv, bgv, wes, wev, bev, out):
    with ExitStack() as ctx:
        def sb(name, shape, dt, where=ctx):
            return where.enter_context(nc.sbuf_tensor(name, shape, dt))

        def sem(name):
            return ctx.enter_context(nc.semaphore(name))

        kt_hi = sb("kt_hi", [P, C, N], F32R)
        kt_lo = sb("kt_lo", [P, C, N], F32R)
        val = sb("val", [P, N // P, 2 * D], F32R)
        ident = sb("ident", [P, P], F32)
        we_hi = sb("we_hi", [P, C, D + 2], F32R)
        we_lo = sb("we_lo", [P, C, D + 2], F32R)
        bev_all = sb("bev_all", [P, D + 2], F32)
        gv = sb("gv", [P, D], F32)
        minus_half = sb("minus_half", [P, 1], F32)
        adj_in = [sb("adj_in0", [P, N], U8)]
        m_in = sb("m_in", [P, 2, D], F32)
        mt_hi = [sb(f"mt_hi{k}", [P, C, P], F32R) for k in range(2)]
        mt_lo = [sb(f"mt_lo{k}", [P, C, P], F32R) for k in range(2)]

        prep = ExitStack()
        x_in = [sb(f"x_in{k}", [P, SUB, D], F32, prep) for k in range(2)]
        xs_hi = [sb(f"xs_hi{k}", [P, C, KEYS], F32R, prep) for k in range(2)]
        xs_lo = [sb(f"xs_lo{k}", [P, C, KEYS], F32R, prep) for k in range(2)]
        raw = {k: sb(f"raw_{k}", [P, C, D], F32, prep) for k in ("wlq", "wlk", "wlv")}
        wk_t = sb("wk_t", [P, C, D], F32, prep)
        a_hi = sb("a_hi", [P, C, D], F32R, prep)
        a_lo = sb("a_lo", [P, C, D], F32R, prep)
        wv_hi = sb("wv_hi", [P, C, D], F32R, prep)
        wv_lo = sb("wv_lo", [P, C, D], F32R, prep)
        blv_all = sb("blv_all", [P, D], F32, prep)
        v_sum = sb("v_sum", [P, SUB, D], F32, prep)
        wq_t = sb("wq_t", [P, C, D], F32, prep)
        raw.update({k: sb(f"raw_{k}", [P, C, D], F32, prep) for k in ("wgq", "wgk", "wgv")})
        raw["we"] = sb("raw_we", [P, C, D + 2], F32, prep)
        bgv_all = sb("bgv_all", [P, D], F32, prep)
        xsum = sb("xsum", [P, C, BLOCKS], F32, prep)
        xtot = sb("xtot", [P, C], F32, prep)
        xmean = sb("xmean", [P, C, P], F32, prep)
        gk = sb("gk", [P, C], F32, prep)
        prep.close()
        score = [sb(f"score{k}", [P, N], F32) for k in range(2)]
        ev = [sb(f"ev{k}", [P, D + 2 + BLOCKS], F32) for k in range(2)]
        neg_max = [sb(f"neg_max{k}", [P, 1], F32) for k in range(2)]
        parts = [sb(f"parts{k}", [P, PIECES + 2], F32) for k in range(2)]
        adj_in.append(sb("adj_in1", [P, N], U8))
        den = sb("den", [P, 1], F32)
        rden = sb("rden", [P, 1], F32)
        stats = sb("stats", [P, 6], F32)
        mean_var = sb("mean_var", [P, 2], F32)
        var_eps = sb("var_eps", [P, 1], F32)
        rstd = sb("rstd", [P, 1], F32)
        acc = sb("acc", [P, D], F32)
        y = [sb(f"y{k}", [P, D], F32) for k in range(2)]
        pt_hi = [sb(f"pt_hi{k}", [P, KEYS], F32R) for k in range(2)]
        pt_lo = [sb(f"pt_lo{k}", [P, KEYS], F32R) for k in range(2)]
        fin_in = [sb(f"fin_in{k}", [P, 2, D], F32) for k in range(2)]

        ps = ctx.enter_context(nc.psum_tensor("ps", [P, 8, KEYS], F32))

        consts_ready = sem("consts_ready")
        wl_loaded = sem("wl_loaded")
        wv_loaded = sem("wv_loaded")
        wg_loaded = sem("wg_loaded")
        x_loaded = [sem(f"x_loaded{k}") for k in range(2)]
        prep_pe = sem("prep_pe")
        prep_dve = sem("prep_dve")
        xt_ready = sem("xt_ready")
        xs_hi_ready = sem("xs_hi_ready")
        xs_ready = sem("xs_ready")
        v_ready = sem("v_ready")
        v_summed = sem("v_summed")
        v_hi_ready = sem("v_hi_ready")
        v_split = sem("v_split")
        k_ready = sem("k_ready")
        k_hi_ready = sem("k_hi_ready")
        k_split = sem("k_split")
        adj_loaded = [sem(f"adj_loaded{k}") for k in range(2)]
        m_loaded = sem("m_loaded")
        fin_loaded = [sem(f"fin_loaded{k}") for k in range(2)]
        out_stored = [sem(f"out_stored{k}") for k in range(2)]
        bias_ready = sem("bias_ready")
        s_ready = sem("s_ready")
        s_masked = sem("s_masked")
        max_ready = sem("max_ready")
        exp_ready = sem("exp_ready")
        ge_ready = sem("ge_ready")
        t_ready = sem("t_ready")
        pt_hi_ready = sem("pt_hi_ready")
        pt_ready = sem("pt_ready")
        pv_done = sem("pv_done")
        mt_ready = sem("mt_ready")
        mt_hi_ready = sem("mt_hi_ready")
        mt_split = sem("mt_split")
        e_ready = sem("e_ready")
        e_copied = sem("e_copied")
        den_ready = sem("den_ready")
        rden_ready = sem("rden_ready")
        gv_added = sem("gv_added")
        o_used = sem("o_used")
        ev_used = sem("ev_used")
        res_ready = sem("res_ready")
        fin_used = sem("fin_used")
        stats_ready = sem("stats_ready")
        mean_ready = sem("mean_ready")
        y_ready = sem("y_ready")
        var_ready = sem("var_ready")
        rstd_ready = sem("rstd_ready")

        block = ctx.enter_context(nc.Block())

        x_blocks = x.rearrange("(b a p) d -> b p a d", a=SUB, p=P)
        m_pairs = masked_x.rearrange("(i a p) d -> i p a d", a=2, p=P)
        m_tiles = masked_x.rearrange("(t p) d -> t p d", p=P)
        x_tiles = x.rearrange("(t p) d -> t p d", p=P)
        adj_tiles = adj.rearrange("(t p) n -> t p n", p=P)
        out_tiles = out.rearrange("(t p) d -> t p d", p=P)

        def rows_by_chunk(w):
            return w.rearrange("(r p) n -> p r n", p=P)

        def one_row(b):
            return b.rearrange("(a n) -> a n", a=1)

        @block.sync
        def _(sp):
            def load_x(b, par, i):
                sp.dma_start(x_in[par][:], x_blocks[b]).then_inc(x_loaded[par], 16)

            sp.dma_start(raw["wlq"][:], rows_by_chunk(wlq)).then_inc(wl_loaded, 16)
            sp.dma_start(raw["wlk"][:], rows_by_chunk(wlk)).then_inc(wl_loaded, 16)
            sp.dma_start(m_in[:], m_pairs[0]).then_inc(m_loaded, 16)
            load_x(0, 0, 0)
            sp.dma_start(raw["wlv"][:], rows_by_chunk(wlv)).then_inc(wv_loaded, 16)
            sp.dma_start(blv_all[:], one_row(blv).to_broadcast([P, D])).then_inc(wv_loaded, 16)
            sp.dma_start(bev_all[:, 0:D], one_row(bev).to_broadcast([P, D])).then_inc(wv_loaded, 16)
            load_x(1, 1, 0)
            for name, w in (("wgq", wgq), ("wgk", wgk), ("wgv", wgv)):
                sp.dma_start(raw[name][:], rows_by_chunk(w)).then_inc(wg_loaded, 16)
            sp.dma_start(raw["we"][:, :, 0:D], rows_by_chunk(wev)).then_inc(wg_loaded, 16)
            with nc.allow_non_contiguous_dma(reason="one column"):
                sp.dma_start(raw["we"][:, :, D + 1:D + 2], rows_by_chunk(wes)).then_inc(wg_loaded, 16)
            sp.dma_start(bgv_all[:], one_row(bgv).to_broadcast([P, D])).then_inc(wg_loaded, 16)
            with sp.Fori(0, BLOCKS // 2 - 1) as i:
                for par in range(2):
                    sp.wait_ge(xt_ready, 2 * i + par + 1)
                    load_x(2 * i + par + 2, par, i)
            sp.dma_start(adj_in[0][:], adj_tiles[0]).then_inc(adj_loaded[0], 16)
            sp.wait_ge(k_split, BLOCKS)
            sp.dma_start(adj_in[1][:], adj_tiles[1]).then_inc(adj_loaded[1], 16)

            def tile(i, par):
                t = 2 * i + par
                if exists(i + 1):
                    at_least(sp, bias_ready, PIECES * (t + 1))
                    sp.dma_start(adj_in[par][:], adj_tiles[t + 2]).then_inc(adj_loaded[par], 16)
                    if par == 0:
                        sp.wait_ge(mt_ready, i + 1)
                        sp.dma_start(m_in[:], m_pairs[i + 1]).then_inc(m_loaded, 16)
                if exists(i):
                    if isinstance(i, int) and t == 0:
                        sp.wait_ge(prep_dve, PREP_DVE)
                    at_least(sp, fin_used, t - 1)
                    sp.dma_start(fin_in[par][:, 0, :], m_tiles[t]).then_inc(fin_loaded[par], 16)
                    sp.dma_start(fin_in[par][:, 1, :], x_tiles[t]).then_inc(fin_loaded[par], 16)
                if exists(i - 1):
                    sp.wait_ge(y_ready, t - 1)
                    sp.dma_start(out_tiles[t - 2], y[par][:]).then_inc(out_stored[par], 16)

            for i in range(1):
                tile(i, 0)
                tile(i, 1)
            with sp.Fori(1, PAIRS - 1) as i:
                tile(i, 0)
                tile(i, 1)
            for i in (PAIRS - 1, PAIRS):
                tile(i, 0)
                tile(i, 1)
            for par in range(2):
                sp.wait_ge(out_stored[par], 16 * (PAIRS + 1))

        @block.gpsimd
        def _(gp):
            gp.memset(ident[:], 0.0).then_inc(consts_ready, 1)
            gp.wait_ge(consts_ready, 1)
            gp.affine_select(out=ident[:], in_=ident[:], compare_op=ALU.not_equal, fill=1.0, base=0,
                             pattern=[[-1, P]], channel_multiplier=1).then_inc(consts_ready, 1)
            gp.memset(minus_half[:], -0.5).then_inc(consts_ready, 1)
            gp.memset(bev_all[:, D:D + 2], 0.0).then_inc(consts_ready, 1)

            def bias(i, par, piece):
                t = 2 * i + par
                if piece == 0:
                    gp.wait_ge(adj_loaded[par], 16 * (i + 1))
                cols = slice(piece * PIECE, (piece + 1) * PIECE)
                if not isinstance(i, int) or i > 0:
                    gp.wait_ge(t_ready, BLOCKS * (t - 2) + (piece + 1) * BLOCKS // PIECES)
                elif piece == 0 and par == 0:
                    gp.wait_ge(k_split, BLOCKS)
                keep_apart(gp)
                gp.tensor_scalar(score[par][:, cols], adj_in[par][:, cols], -1.0, MASKED,
                                 ALU.add, ALU.mult).then_inc(bias_ready, 1)

            def inverse_deviation(i, par):
                t = 2 * i + par
                gp.wait_ge(mean_ready, t + 1)
                keep_apart(gp)
                gp.tensor_scalar(var_eps[:], mean_var[:, 1:2], EPS, 1.0, ALU.add,
                                 ALU.mult).then_inc(var_ready, 1)
                gp.wait_ge(var_ready, t + 1)
                gp.tensor_tensor(rstd[:], var_eps[:], minus_half[:], ALU.pow).then_inc(rstd_ready, 1)

            def tile(i, par):
                ni, npar = back(i, par, -1)
                fi, fpar = back(i, par, 2)
                if exists(ni):
                    bias(ni, npar, 0)
                    bias(ni, npar, 1)
                if exists(fi):
                    inverse_deviation(fi, fpar)
                if exists(ni):
                    bias(ni, npar, 2)
                    bias(ni, npar, 3)

            for piece in range(PIECES):
                bias(0, 0, piece)
            tile(0, 0)
            tile(0, 1)
            with gp.Fori(1, PAIRS - 1) as i:
                tile(i, 0)
                tile(i, 1)
            for i in (PAIRS - 1, PAIRS):
                tile(i, 0)
                tile(i, 1)

        @block.tensor
        def _(pe):
            def three_passes(o, w_hi, w_lo, m_hi, m_lo, start, stop):
                pe.matmul(o, w_hi, m_hi, start=start, stop=False, skip_group_check=True)
                pe.matmul(o, w_hi, m_lo, start=False, stop=False, skip_group_check=True)
                return pe.matmul(o, w_lo, m_hi, start=False, stop=stop, skip_group_check=True)

            def transpose_weight(w, bank):
                for cc in range(C):
                    for r in range(C):
                        last = pe.transpose(ps[:, bank, cc * D + r * P:cc * D + (r + 1) * P],
                                            w[:, r, cc * P:(cc + 1) * P], ident[:])
                return last

            def transpose_masked_x(i):
                pe.wait_ge(m_loaded, 16 * (i + 1))
                at_least(pe, mt_split, 2 * i)
                for cc in range(C):
                    for a in range(2):
                        last = pe.transpose(ps[:, M_BANK, cc * D + a * P:cc * D + (a + 1) * P],
                                            m_in[:, a, cc * P:(cc + 1) * P], ident[:])
                last.then_inc(mt_ready, 1)

            pe.wait_ge(consts_ready, 2)
            pe.wait_ge(wl_loaded, 32)
            transpose_weight(raw["wlq"], 4)
            transpose_weight(raw["wlk"], 5).then_inc(prep_pe, 1)
            transpose_masked_x(0)

            def x_transpose(b, par, i):
                pe.wait_ge(x_loaded[par], 16 * (i + 1))
                at_least(pe, xs_ready, b - 1)
                for cc in range(C):
                    for a in range(SUB):
                        last = pe.transpose(ps[:, 2 * par + cc, a * P:(a + 1) * P],
                                            x_in[par][:, a, cc * P:(cc + 1) * P], ident[:])
                last.then_inc(xt_ready, 1)

            def values(b, par):
                pe.wait_ge(xs_ready, b + 1)
                at_least(pe, v_summed, b)
                for a in range(SUB):
                    o = ps[:, O_BANK + a // 2, (a % 2) * D:(a % 2 + 1) * D]
                    rows = slice(a * P, (a + 1) * P)
                    for cc in range(C):
                        last = three_passes(o, xs_hi[par][:, cc, rows], xs_lo[par][:, cc, rows],
                                            wv_hi[:, cc, :], wv_lo[:, cc, :], cc == 0, cc == C - 1)
                last.then_inc(v_ready, 1)

            def keys(b, par):
                at_least(pe, k_split, b)
                for oc in range(C):
                    for cc in range(C):
                        cols = slice(oc * P, (oc + 1) * P)
                        last = three_passes(ps[:, M_BANK + oc, :], a_hi[:, cc, cols], a_lo[:, cc, cols],
                                            xs_hi[par][:, cc, :], xs_lo[par][:, cc, :], cc == 0,
                                            cc == C - 1)
                last.then_inc(k_ready, 1)

            x_transpose(0, 0, 0)
            pe.wait_ge(prep_dve, DVE_WT)
            for r in range(C):
                for cc in range(C):
                    last = pe.matmul(ps[:, 7, r * D:(r + 1) * D], wk_t[:, cc, r * P:(r + 1) * P],
                                     wq_t[:, cc, :], start=(cc == 0), stop=(cc == C - 1))
            last.then_inc(prep_pe, 1)
            pe.wait_ge(prep_dve, DVE_WV)
            x_transpose(1, 1, 0)
            values(0, 0)
            pe.wait_ge(prep_dve, DVE_A)
            pe.wait_ge(mt_split, 2)
            keys(0, 0)
            with pe.Fori(0, BLOCKS // 2 - 1) as i:
                x_transpose(2 * i + 2, 0, i + 1)
                values(2 * i + 1, 1)
                keys(2 * i + 1, 1)
                x_transpose(2 * i + 3, 1, i + 1)
                values(2 * i + 2, 0)
                keys(2 * i + 2, 0)
            values(BLOCKS - 1, 1)
            keys(BLOCKS - 1, 1)

            def global_key(j):
                if j == 0:
                    pe.wait_ge(wg_loaded, 16 * 6)
                    transpose_weight(raw["wgq"], 2)
                    pe.wait_ge(prep_dve, DVE_MEAN)
                    pe.wait_ge(v_split, BLOCKS)
                    for oc in range(C):
                        for cc in range(C):
                            pe.matmul(ps[:, 4, oc:oc + 1], raw["wgk"][:, cc, oc * P:(oc + 1) * P],
                                      xmean[:, cc, 0:1], start=(cc == 0), stop=(cc == C - 1))
                    for cc in range(C):
                        last = pe.matmul(ps[:, 5, 0:D], xmean[:, cc, :], raw["wgv"][:, cc, :],
                                         start=(cc == 0), stop=(cc == C - 1))
                    last.then_inc(prep_pe, 1)
                if j == 2:
                    pe.wait_ge(prep_dve, DVE_GK)
                    for oc in range(C):
                        for cc in range(C):
                            last = pe.matmul(ps[:, 3, oc:oc + 1], wq_t[:, cc, oc * P:(oc + 1) * P],
                                             gk[:, cc:cc + 1], start=(cc == 0), stop=(cc == C - 1))
                    last.then_inc(prep_pe, 1)

            def scores(i, par, j):
                s = 2 * BLOCKS * i + BLOCKS * par + j
                if j == 0:
                    pe.wait_ge(mt_split, 2 * i + par + 1)
                if isinstance(i, int) and i == 0 and par == 0:
                    pe.wait_ge(k_split, BLOCKS)
                at_least(pe, s_masked, s - 1)
                for cc in range(C):
                    block_keys = slice(j * KEYS, (j + 1) * KEYS)
                    last = three_passes(ps[:, S_BANK + j % 2, :], mt_hi[par][:, cc, :],
                                        mt_lo[par][:, cc, :], kt_hi[:, cc, block_keys],
                                        kt_lo[:, cc, block_keys], cc == 0, cc == C - 1)
                last.then_inc(s_ready, 1)

            def transpose_weights(i, par, g):
                u = 2 * BLOCKS * i + BLOCKS * par + g
                if g % 2 == 0:
                    pe.wait_ge(exp_ready, PIECES * (2 * i + par) + g * PIECES // BLOCKS + 1)
                at_least(pe, pt_ready, u - 1)
                for k in range(SUB):
                    last = pe.transpose(ps[:, T_BANK + g % 2, k * P:(k + 1) * P],
                                        score[par][:, g * KEYS + k * P:g * KEYS + (k + 1) * P],
                                        ident[:])
                last.then_inc(t_ready, 1)

            def weigh_values(i, par, g):
                u = 2 * BLOCKS * i + BLOCKS * par + g
                pe.wait_ge(pt_ready, u + 1)
                if g == 0:
                    at_least(pe, o_used, 2 * i + par)
                for k in range(SUB):
                    chunk = g * SUB + k
                    w = slice(k * P, (k + 1) * P)
                    pe.matmul(ps[:, O_BANK + par, :], pt_hi[g % 2][:, w], val[:, chunk, :],
                              start=(chunk == 0), stop=False, skip_group_check=True)
                    last = pe.matmul(ps[:, O_BANK + par, 0:D], pt_lo[g % 2][:, w], val[:, chunk, 0:D],
                                     start=False, stop=(chunk == N // P - 1), skip_group_check=True)
                last.then_inc(pv_done, 1)

            def self_values(i, par):
                if isinstance(i, int) and i == 0 and par == 0:
                    pe.wait_ge(prep_dve, PREP_DVE)
                at_least(pe, e_copied, 2 * i + par)
                for cc in range(C):
                    last = three_passes(ps[:, E_BANK, 0:D + 2], mt_hi[par][:, cc, :],
                                        mt_lo[par][:, cc, :], we_hi[:, cc, :], we_lo[:, cc, :],
                                        cc == 0, cc == C - 1)
                last.then_inc(e_ready, 1)

            def slot(i, par, j):
                if exists(i):
                    scores(i, par, j)
                ti, tpar = back(i, par, 1 if j >= 1 else 2)
                if exists(ti):
                    transpose_weights(ti, tpar, (j - 1) % BLOCKS)
                vi, vpar = back(i, par, 1 if j >= 2 else 2)
                if exists(vi):
                    weigh_values(vi, vpar, (j - 2) % BLOCKS)
                if isinstance(i, int) and i == 0 and par == 0:
                    global_key(j)
                if j == 4 and exists(i):
                    self_values(i, par)
                if par == 1 and j == 5 and exists(i) and exists(i + 1):
                    transpose_masked_x(i + 1)

            def pair(i):
                for par in range(2):
                    for j in range(BLOCKS):
                        slot(i, par, j)

            pair(0)
            with pe.Fori(1, PAIRS - 1) as i:
                pair(i)
            pair(PAIRS - 1)
            pair(PAIRS)

        @block.scalar
        def _(act):
            def x_hi(b, par):
                act.wait_ge(xt_ready, b + 1)
                at_least(act, k_ready, b - 1)
                for cc in range(C):
                    last = act.activation(xs_hi[par][:, cc, :], ps[:, 2 * par + cc, :], ACT.Copy,
                                          accum_out=xsum[:, cc, bass.ds(b, 1)])
                last.then_inc(xs_hi_ready, 1)

            def v_hi(b, par):
                act.wait_ge(v_summed, b + 1)
                act.activation(val[:, bass.ds(b * SUB, SUB), 0:D], v_sum[:],
                               ACT.Copy).then_inc(v_hi_ready, 1)

            def k_hi(b, par):
                act.wait_ge(k_ready, b + 1)
                act.activation(kt_hi[:, :, bass.ds(b * KEYS, KEYS)], ps[:, M_BANK:M_BANK + 2, :],
                               ACT.Copy).then_inc(k_hi_ready, 1)

            x_hi(0, 0)
            x_hi(1, 1)
            v_hi(0, 0)
            k_hi(0, 0)
            with act.Fori(0, BLOCKS // 2 - 1) as i:
                x_hi(2 * i + 2, 0)
                v_hi(2 * i + 1, 1)
                k_hi(2 * i + 1, 1)
                x_hi(2 * i + 3, 1)
                v_hi(2 * i + 2, 0)
                k_hi(2 * i + 2, 0)
            v_hi(BLOCKS - 1, 1)
            k_hi(BLOCKS - 1, 1)

            def exps(i, par, piece):
                t = 2 * i + par
                if piece == 0:
                    act.wait_ge(max_ready, t + 1)
                    at_least(act, ev_used, t)
                    act.activation(parts[par][:, PIECES:PIECES + 2], ev[par][:, D:D + 2], ACT.Exp,
                                   bias=neg_max[par][:]).then_inc(ge_ready, 1)
                cols = slice(piece * PIECE, (piece + 1) * PIECE)
                act.activation(score[par][:, cols], score[par][:, cols], ACT.Exp,
                               bias=neg_max[par][:],
                               accum_out=parts[par][:, piece:piece + 1]).then_inc(exp_ready, 1)

            def weights_hi(i, par, g):
                u = 2 * BLOCKS * i + BLOCKS * par + g
                act.wait_ge(t_ready, u + 1)
                at_least(act, pv_done, u - 1)
                act.activation(pt_hi[g % 2][:], ps[:, T_BANK + g % 2, :],
                               ACT.Copy).then_inc(pt_hi_ready, 1)

            def slot(i, par, j):
                pi, ppar = back(i, par, 1)
                if j < PIECES and exists(pi):
                    exps(pi, ppar, j)
                ti, tpar = back(i, par, 1 if j >= 1 else 2)
                if exists(ti):
                    weights_hi(ti, tpar, (j - 1) % BLOCKS)

            def pair(i):
                for par in range(2):
                    for j in range(BLOCKS):
                        slot(i, par, j)

            pair(0)
            with act.Fori(1, PAIRS - 1) as i:
                pair(i)
            pair(PAIRS - 1)
            pair(PAIRS)

        @block.vector
        def _(dve):
            def split_masked_x(i, par):
                t = 2 * i + par
                mine = ps[:, M_BANK, :].rearrange("p (c n) -> p c n", c=C)[:, :, par * P:(par + 1) * P]
                dve.wait_ge(mt_ready, i + 1)
                if not isinstance(i, int) or i > 0:
                    dve.wait_ge(s_ready, BLOCKS * (t - 1))
                dve.tensor_copy(mt_hi[par][:], mine).then_inc(mt_hi_ready, 1)
                dve.wait_ge(mt_hi_ready, t + 1)
                dve.tensor_tensor(mt_lo[par][:], mine, mt_hi[par][:].bitcast(F32),
                                  ALU.subtract).then_inc(mt_split, 1)

            dve.memset(xtot[:, 0:1], 0.0).then_inc(o_used, 1)
            dve.memset(xtot[:, 1:2], 0.0).then_inc(ev_used, 1)
            for k in range(2):
                dve.memset(gk[:, k:k + 1], 0.0).then_inc(out_stored[k], 16)

            steps = [0]

            def step(ins):
                steps[0] += 1
                ins.then_inc(prep_dve, 1)
                dve.wait_ge(prep_dve, steps[0])

            def at(mark):
                assert steps[0] == mark, (steps[0], mark)

            two = "p (c n) -> p c n"
            dve.wait_ge(prep_pe, 1)
            step(dve.tensor_copy(wq_t[:], ps[:, 4, :].rearrange(two, c=C)))
            step(dve.tensor_copy(wk_t[:], ps[:, 5, :].rearrange(two, c=C)))
            at(DVE_WT)
            dve.wait_ge(wv_loaded, 16 * 3)
            step(dve.tensor_copy(wv_hi[:], raw["wlv"][:]))
            step(dve.tensor_tensor(wv_lo[:], raw["wlv"][:], wv_hi[:].bitcast(F32), ALU.subtract))
            at(DVE_WV)

            def x_lo(b, par):
                dve.wait_ge(xs_hi_ready, b + 1)
                dve.tensor_tensor(xs_lo[par][:], ps[:, 2 * par:2 * par + 2, :],
                                  xs_hi[par][:].bitcast(F32), ALU.subtract).then_inc(xs_ready, 1)

            def v_add(b):
                dve.wait_ge(v_ready, b + 1)
                at_least(dve, v_split, b)
                dve.tensor_tensor(v_sum[:].rearrange("p (b a) n -> p b a n", a=2),
                                  ps[:, O_BANK:O_BANK + 2, :].rearrange("p b (a n) -> p b a n", a=2),
                                  blv_all[:].unsqueeze(1).unsqueeze(1).to_broadcast([P, 2, 2, D]),
                                  ALU.add).then_inc(v_summed, 1)

            def v_lo(b):
                dve.wait_ge(v_hi_ready, b + 1)
                chunks = bass.ds(b * SUB, SUB)
                dve.tensor_tensor(val[:, chunks, D:2 * D], v_sum[:], val[:, chunks, 0:D].bitcast(F32),
                                  ALU.subtract).then_inc(v_split, 1)

            def k_lo(b):
                dve.wait_ge(k_hi_ready, b + 1)
                cols = bass.ds(b * KEYS, KEYS)
                dve.tensor_tensor(kt_lo[:, :, cols], ps[:, M_BANK:M_BANK + 2, :],
                                  kt_hi[:, :, cols].bitcast(F32), ALU.subtract).then_inc(k_split, 1)

            x_lo(0, 0)
            dve.wait_ge(prep_pe, 2)
            a_psum = ps[:, 7, :].rearrange(two, c=C)
            step(dve.tensor_scalar(a_hi[:], a_psum, SCALE, None, ALU.mult))
            step(dve.scalar_tensor_tensor(a_lo[:], a_psum, SCALE, a_hi[:].bitcast(F32), ALU.mult,
                                          ALU.subtract))
            at(DVE_A)
            split_masked_x(0, 0)
            split_masked_x(0, 1)
            x_lo(1, 1)
            v_add(0)
            v_lo(0)
            k_lo(0)
            with dve.Fori(0, BLOCKS // 2 - 1) as i:
                x_lo(2 * i + 2, 0)
                v_add(2 * i + 1)
                v_lo(2 * i + 1)
                k_lo(2 * i + 1)
                x_lo(2 * i + 3, 1)
                v_add(2 * i + 2)
                v_lo(2 * i + 2)
                k_lo(2 * i + 2)
            v_add(BLOCKS - 1)
            v_lo(BLOCKS - 1)
            k_lo(BLOCKS - 1)

            def global_key(j):
                if j == 0:
                    step(dve.tensor_reduce(xtot[:], xsum[:], AX_X, ALU.add))
                    for cc in range(C):
                        step(dve.tensor_scalar(xmean[:, cc, :], xtot[:, cc:cc + 1].to_broadcast([P, P]),
                                               1.0 / N, None, ALU.mult))
                    at(DVE_MEAN)
                if j == 1:
                    dve.wait_ge(prep_pe, 3)
                    step(dve.tensor_copy(wq_t[:], ps[:, 2, :].rearrange(two, c=C)))
                    step(dve.tensor_copy(gk[:], ps[:, 4, 0:C]))
                    at(DVE_GK)
                    step(dve.tensor_tensor(gv[:], ps[:, 5, 0:D], bgv_all[:], ALU.add))
                if j == 3:
                    dve.wait_ge(prep_pe, 4)
                    step(dve.tensor_scalar(raw["we"][:, :, D:D + 1], ps[:, 3, 0:C].rearrange(
                        "p (c n) -> p c n", n=1), SCALE, None, ALU.mult))
                    step(dve.tensor_copy(we_hi[:], raw["we"][:]))
                    step(dve.tensor_tensor(we_lo[:], raw["we"][:], we_hi[:].bitcast(F32),
                                           ALU.subtract))
                    at(PREP_DVE)

            def mask_scores(i, par, j):
                s = 2 * BLOCKS * i + BLOCKS * par + j
                dve.wait_ge(s_ready, s + 1)
                if j % 2 == 0:
                    dve.wait_ge(bias_ready, PIECES * (2 * i + par) + j * PIECES // BLOCKS + 1)
                keep_apart(dve)
                mine = score[par][:, j * KEYS:(j + 1) * KEYS]
                dve.tensor_tensor_reduce(mine, ps[:, S_BANK + j % 2, :], mine, 1.0, LOWEST, ALU.add,
                                         ALU.max, ev[par][:, D + 2 + j:D + 3 + j]).then_inc(s_masked, 1)

            def row_max(i, par):
                t = 2 * i + par
                dve.wait_ge(s_masked, BLOCKS * (t + 1))
                dve.wait_ge(e_copied, t + 1)
                dve.tensor_reduce(neg_max[par][:], ev[par][:, D:], AX_X, ALU.max,
                                  negate=True).then_inc(max_ready, 1)

            def add_self_bias(i, par):
                t = 2 * i + par
                dve.wait_ge(e_ready, t + 1)
                at_least(dve, ev_used, t)
                dve.tensor_tensor(ev[par][:, 0:D + 2], ps[:, E_BANK, 0:D + 2], bev_all[:],
                                  ALU.add).then_inc(e_copied, 1)

            def weights_lo(i, par, g):
                u = 2 * BLOCKS * i + BLOCKS * par + g
                dve.wait_ge(pt_hi_ready, u + 1)
                dve.tensor_tensor(pt_lo[g % 2][:], ps[:, T_BANK + g % 2, :],
                                  pt_hi[g % 2][:].bitcast(F32), ALU.subtract).then_inc(pt_ready, 1)

            def finish(i, par, j):
                t = 2 * i + par
                o = ps[:, O_BANK + par, :]
                m_row, x_row = fin_in[par][:, 0, :], fin_in[par][:, 1, :]
                if j == 2:
                    dve.wait_ge(exp_ready, PIECES * (t + 1))
                    dve.tensor_reduce(den[:], parts[par][:], AX_X, ALU.add).then_inc(den_ready, 1)
                    dve.wait_ge(den_ready, t + 1)
                    dve.reciprocal(rden[:], den[:]).then_inc(rden_ready, 1)
                    dve.wait_ge(pv_done, BLOCKS * (t + 1))
                    dve.scalar_tensor_tensor(acc[:], gv[:], parts[par][:, PIECES:PIECES + 1],
                                             o[:, 0:D], ALU.mult, ALU.add).then_inc(gv_added, 1)
                    dve.wait_ge(gv_added, t + 1)
                    dve.tensor_tensor(acc[:], o[:, D:2 * D], acc[:], ALU.add).then_inc(o_used, 1)
                if j == 3:
                    dve.wait_ge(o_used, t + 2)
                    dve.scalar_tensor_tensor(acc[:], ev[par][:, 0:D], parts[par][:, PIECES + 1:PIECES + 2],
                                             acc[:], ALU.mult, ALU.add).then_inc(ev_used, 1)
                    dve.wait_ge(ev_used, t + 2)
                    dve.wait_ge(rden_ready, t + 1)
                    dve.wait_ge(fin_loaded[par], 32 * (i + 1))
                    dve.scalar_tensor_tensor(acc[:], acc[:], rden[:], m_row, ALU.mult,
                                             ALU.max).then_inc(res_ready, 1)
                    dve.wait_ge(res_ready, t + 1)
                    dve.tensor_tensor(acc[:], acc[:], x_row, ALU.add).then_inc(fin_used, 1)
                if j == 4:
                    dve.wait_ge(fin_used, t + 1)
                    dve.bn_stats(stats[:], acc[:]).then_inc(stats_ready, 1)
                    dve.wait_ge(stats_ready, t + 1)
                    keep_apart(dve)
                    dve.bn_aggr(mean_var[:], stats[:]).then_inc(mean_ready, 1)
                if j == 6:
                    dve.wait_ge(rstd_ready, t + 1)
                    at_least(dve, out_stored[par], 16 * (i + 1))
                    dve.tensor_scalar(y[par][:], acc[:], mean_var[:, 0:1], rstd[:], ALU.subtract,
                                      ALU.mult).then_inc(y_ready, 1)

            def slot(i, par, j):
                if isinstance(i, int) and i == 0 and par == 0:
                    global_key(j)
                if par == 1 and j == 7 and exists(i) and exists(i + 1):
                    split_masked_x(i + 1, 0)
                if par == 0 and j == 1 and exists(i) and not (isinstance(i, int) and i == 0):
                    split_masked_x(i, 1)
                if exists(i):
                    mask_scores(i, par, j)
                    if j == BLOCKS - 1:
                        row_max(i, par)
                ti, tpar = back(i, par, 1 if j >= 1 else 2)
                if exists(ti):
                    weights_lo(ti, tpar, (j - 1) % BLOCKS)
                if j == 5 and exists(i):
                    add_self_bias(i, par)
                fi, fpar = back(i, par, 2)
                if exists(fi):
                    finish(fi, fpar, j)

            def pair(i):
                for par in range(2):
                    for j in range(BLOCKS):
                        slot(i, par, j)

            pair(0)
            with dve.Fori(1, PAIRS - 1) as i:
                pair(i)
            pair(PAIRS - 1)
            pair(PAIRS)


DVE_WT = 2
DVE_WV = 4
DVE_A = 6
DVE_MEAN = 9
DVE_GK = 11
PREP_DVE = 15


_INS = ['x', 'adj', 'L0_gnn_masked_x', 'L0_gnn_Wlq', 'L0_gnn_Wlk', 'L0_gnn_Wlv', 'L0_gnn_blv',
        'L0_gnn_Wgq', 'L0_gnn_Wgk', 'L0_gnn_Wgv', 'L0_gnn_bgv', 'L0_gnn_Wes', 'L0_gnn_Wev', 'L0_gnn_bev']


def kernel(**inputs):
    import numpy as _np
    import concourse.bacc as _bacc
    from concourse import mybir as _mybir
    from concourse.bass_utils import run_bass_kernel_spmd as _run

    nc = _bacc.Bacc("TRN2", target_bir_lowering=False, num_devices=1)
    arrays, args = {}, []
    for name in _INS:
        a = _np.ascontiguousarray(inputs[name])
        arrays[f"in_{name}_dram"] = a
        args.append(nc.dram_tensor(f"in_{name}_dram", a.shape, _mybir.dt.from_np(a.dtype), kind="ExternalInput").ap())
    o = nc.dram_tensor("out_0_dram", (N, D), F32, kind="ExternalOutput").ap()
    gnn_resnorm(nc, *args, o)
    r = _run(nc, [arrays], core_ids=[0])
    return r.results[0]["out_0_dram"]
```

```python
from contextlib import ExitStack

import concourse.bass as bass
from concourse import mybir
from concourse.alu_op_type import AluOpType as ALU

F32 = mybir.dt.float32
F32R = mybir.dt.float32r
U8 = mybir.dt.uint8
ACT = mybir.ActivationFunctionType
AX_X = mybir.AxisListType.X

P = 128
N = 4096
D = 256
C = D // P
TILES = N // P
PAIRS = TILES // 2
KEYS = 512
BLOCKS = N // KEYS
SUB = KEYS // P
EDGES = (0, 2, 4, 6, 8)
PIECES = len(EDGES) - 1
B = 32
QUADS = P // B
MOVED = 6
STAYED = BLOCKS - MOVED
MOVED_KEYS = MOVED * KEYS
MOVED_PIECES = PIECES - EDGES.index(STAYED)
PIECE_ORDER = ((1, 2, 3), (0,))
HALVES = 2
HALF = MOVED // HALVES
MOVES = 16 * QUADS * (QUADS - 1)
SCALE = D ** -0.5
MASKED = 1.0e9
LOWEST = -3.0e38
EPS = 1.0e-5

S_BANK, T_BANK, O_BANK, M_BANK, E_BANK = 0, 2, 4, 6, 7


def back(i, par, n):
    return i - (n + 1 - par) // 2, (par - n) % 2


def exists(i):
    return not isinstance(i, int) or 0 <= i < PAIRS


def at_least(engine, semaphore, value):
    if not isinstance(value, int) or value > 0:
        engine.wait_ge(semaphore, value)


def piece_keys(piece):
    return slice(EDGES[piece] * KEYS, EDGES[piece + 1] * KEYS)


def is_last(i, par):
    return isinstance(i, int) and (i, par) == (PAIRS - 1, 1)


def stayed(i, par):
    return BLOCKS if is_last(i, par) else STAYED


def pieces_in_slot(i, par, j):
    if is_last(i, par):
        return (j,) if j < PIECES else ()
    return PIECE_ORDER[j] if j < len(PIECE_ORDER) else ()


def exps_before(i, par, piece):
    order = [p for j in range(BLOCKS) for p in pieces_in_slot(i, par, j)]
    return order.index(piece) + 1


def keep_apart(engine):
    engine.nop(nofuse=True)


def gnn_resnorm(nc, x, adj, masked_x, wlq, wlk, wlv, blv, wgq, wgk, wgv, bgv, wes, wev, bev, out):
    with ExitStack() as ctx:
        def sb(name, shape, dt, where=ctx):
            return where.enter_context(nc.sbuf_tensor(name, shape, dt))

        def sem(name):
            return ctx.enter_context(nc.semaphore(name))

        kt_hi = sb("kt_hi", [P, C, N], F32R)
        kt_lo = sb("kt_lo", [P, C, N], F32R)
        val = sb("val", [P, N // P, 2 * D], F32R)
        ident = sb("ident", [P, P], F32)
        we_hi = sb("we_hi", [P, C, D + 2], F32R)
        we_lo = sb("we_lo", [P, C, D + 2], F32R)
        bev_all = sb("bev_all", [P, D + 2], F32)
        gv = sb("gv", [P, D], F32)
        minus_half = sb("minus_half", [P, 1], F32)
        adj_in = [sb("adj_in0", [P, N], U8)]
        m_in = sb("m_in", [P, 2, D], F32)
        mt_hi = [sb(f"mt_hi{k}", [P, C, P], F32R) for k in range(2)]
        mt_lo = [sb(f"mt_lo{k}", [P, C, P], F32R) for k in range(2)]

        prep = ExitStack()
        x_in = [sb(f"x_in{k}", [P, SUB, D], F32, prep) for k in range(2)]
        xs_hi = [sb(f"xs_hi{k}", [P, C, KEYS], F32R, prep) for k in range(2)]
        xs_lo = [sb(f"xs_lo{k}", [P, C, KEYS], F32R, prep) for k in range(2)]
        raw = {k: sb(f"raw_{k}", [P, C, D], F32, prep) for k in ("wlq", "wlk", "wlv")}
        wk_t = sb("wk_t", [P, C, D], F32, prep)
        a_hi = sb("a_hi", [P, C, D], F32R, prep)
        a_lo = sb("a_lo", [P, C, D], F32R, prep)
        wv_hi = sb("wv_hi", [P, C, D], F32R, prep)
        wv_lo = sb("wv_lo", [P, C, D], F32R, prep)
        blv_all = sb("blv_all", [P, D], F32, prep)
        v_sum = sb("v_sum", [P, SUB, D], F32, prep)
        wq_t = sb("wq_t", [P, C, D], F32, prep)
        raw.update({k: sb(f"raw_{k}", [P, C, D], F32, prep) for k in ("wgq", "wgk", "wgv")})
        raw["we"] = sb("raw_we", [P, C, D + 2], F32, prep)
        bgv_all = sb("bgv_all", [P, D], F32, prep)
        xsum = sb("xsum", [P, C, BLOCKS], F32, prep)
        xtot = sb("xtot", [P, C], F32, prep)
        xmean = sb("xmean", [P, C, P], F32, prep)
        gk = sb("gk", [P, C], F32, prep)
        prep.close()
        score = [sb(f"score{k}", [P, N], F32) for k in range(2)]
        ev = [sb(f"ev{k}", [P, D + 2 + BLOCKS], F32) for k in range(2)]
        neg_max = [sb(f"neg_max{k}", [P, 1], F32) for k in range(2)]
        parts = [sb(f"parts{k}", [P, PIECES + 2], F32) for k in range(2)]
        adj_in.append(sb("adj_in1", [P, N], U8))
        den = sb("den", [P, 1], F32)
        rden = sb("rden", [P, 1], F32)
        stats = sb("stats", [P, 6], F32)
        mean_var = sb("mean_var", [P, 2], F32)
        var_eps = sb("var_eps", [P, 1], F32)
        rstd = sb("rstd", [P, 1], F32)
        acc = sb("acc", [P, D], F32)
        y = sb("y", [P, D], F32)
        pt_hi = [sb(f"pt_hi{k}", [P, KEYS], F32R) for k in range(2)]
        pt_lo = [sb(f"pt_lo{k}", [P, KEYS], F32R) for k in range(2)]
        turned = sb("turned", [P, QUADS, HALVES, HALF * SUB, B], F32)
        fin_in = sb("fin_in", [P, 2, D], F32)

        ps = ctx.enter_context(nc.psum_tensor("ps", [P, 8, KEYS], F32))

        consts_ready = sem("consts_ready")
        wlq_loaded = sem("wlq_loaded")
        wlk_loaded = sem("wlk_loaded")
        wv_loaded = sem("wv_loaded")
        wg_loaded = sem("wg_loaded")
        x_loaded = [sem(f"x_loaded{k}") for k in range(2)]
        prep_pe = sem("prep_pe")
        prep_dve = sem("prep_dve")
        xt_ready = sem("xt_ready")
        xs_hi_ready = sem("xs_hi_ready")
        xs_ready = sem("xs_ready")
        v_ready = sem("v_ready")
        v_summed = sem("v_summed")
        v_hi_ready = sem("v_hi_ready")
        v_split = sem("v_split")
        k_ready = sem("k_ready")
        k_hi_ready = sem("k_hi_ready")
        k_split = sem("k_split")
        adj_loaded = [sem(f"adj_loaded{k}") for k in range(2)]
        m_loaded = sem("m_loaded")
        fin_loaded = sem("fin_loaded")
        out_stored = sem("out_stored")
        bias_ready = sem("bias_ready")
        s_ready = sem("s_ready")
        s_masked = sem("s_masked")
        max_ready = sem("max_ready")
        exp_ready = sem("exp_ready")
        ge_ready = sem("ge_ready")
        turned_ready = sem("turned_ready")
        moved = [sem(f"moved{k}") for k in range(2)]
        kept = sem("kept")
        t_ready = sem("t_ready")
        pt_hi_ready = sem("pt_hi_ready")
        pt_ready = sem("pt_ready")
        pv_done = sem("pv_done")
        mt_ready = sem("mt_ready")
        mt_hi_ready = sem("mt_hi_ready")
        mt_split = sem("mt_split")
        e_ready = sem("e_ready")
        e_copied = sem("e_copied")
        den_ready = sem("den_ready")
        rden_ready = sem("rden_ready")
        gv_added = sem("gv_added")
        o_used = sem("o_used")
        ev_used = sem("ev_used")
        res_ready = sem("res_ready")
        fin_used = sem("fin_used")
        stats_ready = sem("stats_ready")
        mean_ready = sem("mean_ready")
        y_ready = sem("y_ready")
        var_ready = sem("var_ready")
        rstd_ready = sem("rstd_ready")

        block = ctx.enter_context(nc.Block())

        x_blocks = x.rearrange("(b a p) d -> b p a d", a=SUB, p=P)
        m_pairs = masked_x.rearrange("(i a p) d -> i p a d", a=2, p=P)
        m_tiles = masked_x.rearrange("(t p) d -> t p d", p=P)
        x_tiles = x.rearrange("(t p) d -> t p d", p=P)
        adj_tiles = adj.rearrange("(t p) n -> t p n", p=P)
        out_tiles = out.rearrange("(t p) d -> t p d", p=P)

        def rows_by_chunk(w):
            return w.rearrange("(r p) n -> p r n", p=P)

        def one_row(b):
            return b.rearrange("(a n) -> a n", a=1)

        def squares(par):
            return score[par][:, N - MOVED_KEYS:].rearrange("p (h a k q) -> p h a k q", h=HALVES,
                                                            a=QUADS, q=B)

        def transposed(par, g, stays):
            if stays:
                return by_squares(ps[:, T_BANK + g % 2, :])
            half, n = divmod(g - STAYED, HALF)
            return squares(par)[:, half, :, n * SUB:(n + 1) * SUB, :]

        def by_squares(flat):
            return flat.rearrange("p (k a q) -> p a k q", a=QUADS, q=B)

        @block.sync
        def _(sp):
            def load_x(b, par, i):
                sp.dma_start(x_in[par][:], x_blocks[b]).then_inc(x_loaded[par], 16)

            sp.dma_start(raw["wlq"][:], rows_by_chunk(wlq)).then_inc(wlq_loaded, 16)
            sp.dma_start(raw["wlk"][:], rows_by_chunk(wlk)).then_inc(wlk_loaded, 16)
            sp.dma_start(m_in[:], m_pairs[0]).then_inc(m_loaded, 16)
            load_x(0, 0, 0)
            sp.dma_start(raw["wlv"][:], rows_by_chunk(wlv)).then_inc(wv_loaded, 16)
            sp.dma_start(blv_all[:], one_row(blv).to_broadcast([P, D])).then_inc(wv_loaded, 16)
            sp.dma_start(bev_all[:, 0:D], one_row(bev).to_broadcast([P, D])).then_inc(wv_loaded, 16)
            load_x(1, 1, 0)
            for name, w in (("wgq", wgq), ("wgk", wgk), ("wgv", wgv)):
                sp.dma_start(raw[name][:], rows_by_chunk(w)).then_inc(wg_loaded, 16)
            sp.dma_start(raw["we"][:, :, 0:D], rows_by_chunk(wev)).then_inc(wg_loaded, 16)
            with nc.allow_non_contiguous_dma(reason="one column"):
                sp.dma_start(raw["we"][:, :, D + 1:D + 2], rows_by_chunk(wes)).then_inc(wg_loaded, 16)
            sp.dma_start(bgv_all[:], one_row(bgv).to_broadcast([P, D])).then_inc(wg_loaded, 16)
            with sp.Fori(0, BLOCKS // 2 - 1) as i:
                for par in range(2):
                    sp.wait_ge(xt_ready, 2 * i + par + 1)
                    load_x(2 * i + par + 2, par, i)
            sp.dma_start(adj_in[0][:], adj_tiles[0]).then_inc(adj_loaded[0], 16)
            sp.wait_ge(k_split, BLOCKS)
            sp.dma_start(adj_in[1][:], adj_tiles[1]).then_inc(adj_loaded[1], 16)

            def move(i, par):
                sp.wait_ge(turned_ready, MOVED_PIECES * (2 * i + par + 1))
                for shift in range(1, QUADS):
                    for a in range(QUADS):
                        b = (a + shift) % QUADS
                        sp.dma_start(squares(par)[b * B:(b + 1) * B, :, a],
                                     turned[a * B:(a + 1) * B, b]).then_inc(moved[par], 16)

            def tile(i, par):
                t = 2 * i + par
                vi, vpar = back(i, par, 1)
                if exists(vi) and not is_last(vi, vpar):
                    move(vi, vpar)
                if exists(i + 1):
                    at_least(sp, bias_ready, PIECES * (t + 1))
                    sp.dma_start(adj_in[par][:], adj_tiles[t + 2]).then_inc(adj_loaded[par], 16)
                    if par == 0:
                        sp.wait_ge(mt_ready, i + 1)
                        sp.dma_start(m_in[:], m_pairs[i + 1]).then_inc(m_loaded, 16)
                if exists(vi):
                    if isinstance(i, int) and t == 1:
                        sp.wait_ge(prep_dve, PREP_DVE)
                    at_least(sp, fin_used, t - 1)
                    sp.dma_start(fin_in[:, 0, :], m_tiles[t - 1]).then_inc(fin_loaded, 16)
                    sp.dma_start(fin_in[:, 1, :], x_tiles[t - 1]).then_inc(fin_loaded, 16)
                if exists(i - 1):
                    sp.wait_ge(y_ready, t - 1)
                    sp.dma_start(out_tiles[t - 2], y[:]).then_inc(out_stored, 16)

            for i in range(1):
                tile(i, 0)
                tile(i, 1)
            with sp.Fori(1, PAIRS - 1) as i:
                tile(i, 0)
                tile(i, 1)
            for i in (PAIRS - 1, PAIRS):
                tile(i, 0)
                tile(i, 1)
            sp.wait_ge(out_stored, 16 * (TILES + 1))

        @block.gpsimd
        def _(gp):
            gp.memset(ident[:], 0.0).then_inc(consts_ready, 1)
            gp.wait_ge(consts_ready, 1)
            gp.affine_select(out=ident[:], in_=ident[:], compare_op=ALU.not_equal, fill=1.0, base=0,
                             pattern=[[-1, P]], channel_multiplier=1).then_inc(consts_ready, 1)
            gp.memset(minus_half[:], -0.5).then_inc(consts_ready, 1)
            gp.memset(bev_all[:, D:D + 2], 0.0).then_inc(consts_ready, 1)

            def bias(i, par, piece):
                t = 2 * i + par
                if piece == 0:
                    gp.wait_ge(adj_loaded[par], 16 * (i + 1))
                cols = piece_keys(piece)
                if not isinstance(i, int) or i > 0:
                    if piece < PIECES - MOVED_PIECES:
                        gp.wait_ge(t_ready, STAYED * (t - 2) + EDGES[piece + 1])
                    elif EDGES[piece + 1] <= STAYED + HALF:
                        gp.wait_ge(pt_ready, BLOCKS * (t - 2) + STAYED + HALF)
                    else:
                        gp.wait_ge(pt_ready, BLOCKS * (t - 1))
                elif piece == 0 and par == 0:
                    gp.wait_ge(k_split, BLOCKS)
                keep_apart(gp)
                gp.tensor_scalar(score[par][:, cols], adj_in[par][:, cols], -1.0, MASKED,
                                 ALU.add, ALU.mult).then_inc(bias_ready, 1)

            def inverse_deviation(i, par):
                t = 2 * i + par
                gp.wait_ge(mean_ready, t + 1)
                keep_apart(gp)
                gp.tensor_scalar(var_eps[:], mean_var[:, 1:2], EPS, 1.0, ALU.add,
                                 ALU.mult).then_inc(var_ready, 1)
                gp.wait_ge(var_ready, t + 1)
                gp.tensor_tensor(rstd[:], var_eps[:], minus_half[:], ALU.pow).then_inc(rstd_ready, 1)

            def tile(i, par):
                ni, npar = back(i, par, -1)
                fi, fpar = back(i, par, 2)
                if exists(ni):
                    for piece in range(PIECES - MOVED_PIECES):
                        bias(ni, npar, piece)
                if exists(fi):
                    inverse_deviation(fi, fpar)
                if exists(ni):
                    for piece in range(PIECES - MOVED_PIECES, PIECES):
                        bias(ni, npar, piece)

            for piece in range(PIECES):
                bias(0, 0, piece)
            tile(0, 0)
            tile(0, 1)
            with gp.Fori(1, PAIRS - 1) as i:
                tile(i, 0)
                tile(i, 1)
            for i in (PAIRS - 1, PAIRS):
                tile(i, 0)
                tile(i, 1)

        @block.tensor
        def _(pe):
            def three_passes(o, w_hi, w_lo, m_hi, m_lo, start, stop):
                pe.matmul(o, w_hi, m_hi, start=start, stop=False, skip_group_check=True)
                pe.matmul(o, w_hi, m_lo, start=False, stop=False, skip_group_check=True)
                return pe.matmul(o, w_lo, m_hi, start=False, stop=stop, skip_group_check=True)

            def transpose_weight(w, bank):
                for cc in range(C):
                    for r in range(C):
                        last = pe.transpose(ps[:, bank, cc * D + r * P:cc * D + (r + 1) * P],
                                            w[:, r, cc * P:(cc + 1) * P], ident[:])
                return last

            def transpose_masked_x(i):
                pe.wait_ge(m_loaded, 16 * (i + 1))
                at_least(pe, mt_split, 2 * i)
                for cc in range(C):
                    for a in range(2):
                        last = pe.transpose(ps[:, M_BANK, cc * D + a * P:cc * D + (a + 1) * P],
                                            m_in[:, a, cc * P:(cc + 1) * P], ident[:])
                last.then_inc(mt_ready, 1)

            pe.wait_ge(consts_ready, 2)
            pe.wait_ge(wlq_loaded, 16)
            transpose_weight(raw["wlq"], 4)
            pe.wait_ge(wlk_loaded, 16)
            transpose_weight(raw["wlk"], 5).then_inc(prep_pe, 1)
            transpose_masked_x(0)

            def x_transpose(b, par, i):
                pe.wait_ge(x_loaded[par], 16 * (i + 1))
                at_least(pe, xs_ready, b - 1)
                for cc in range(C):
                    for a in range(SUB):
                        last = pe.transpose(ps[:, 2 * par + cc, a * P:(a + 1) * P],
                                            x_in[par][:, a, cc * P:(cc + 1) * P], ident[:])
                last.then_inc(xt_ready, 1)

            def values(b, par):
                pe.wait_ge(xs_ready, b + 1)
                at_least(pe, v_summed, b)
                for a in range(SUB):
                    o = ps[:, O_BANK + a // 2, (a % 2) * D:(a % 2 + 1) * D]
                    rows = slice(a * P, (a + 1) * P)
                    for cc in range(C):
                        last = three_passes(o, xs_hi[par][:, cc, rows], xs_lo[par][:, cc, rows],
                                            wv_hi[:, cc, :], wv_lo[:, cc, :], cc == 0, cc == C - 1)
                last.then_inc(v_ready, 1)

            def keys(b, par):
                at_least(pe, k_split, b)
                for oc in range(C):
                    for cc in range(C):
                        cols = slice(oc * P, (oc + 1) * P)
                        last = three_passes(ps[:, M_BANK + oc, :], a_hi[:, cc, cols], a_lo[:, cc, cols],
                                            xs_hi[par][:, cc, :], xs_lo[par][:, cc, :], cc == 0,
                                            cc == C - 1)
                last.then_inc(k_ready, 1)

            x_transpose(0, 0, 0)
            pe.wait_ge(prep_dve, DVE_WT)
            for r in range(C):
                for cc in range(C):
                    last = pe.matmul(ps[:, 7, r * D:(r + 1) * D], wk_t[:, cc, r * P:(r + 1) * P],
                                     wq_t[:, cc, :], start=(cc == 0), stop=(cc == C - 1))
            last.then_inc(prep_pe, 1)
            pe.wait_ge(prep_dve, DVE_WV)
            x_transpose(1, 1, 0)
            values(0, 0)
            pe.wait_ge(prep_dve, DVE_A)
            pe.wait_ge(mt_split, 2)
            keys(0, 0)
            with pe.Fori(0, BLOCKS // 2 - 1) as i:
                x_transpose(2 * i + 2, 0, i + 1)
                values(2 * i + 1, 1)
                keys(2 * i + 1, 1)
                x_transpose(2 * i + 3, 1, i + 1)
                values(2 * i + 2, 0)
                keys(2 * i + 2, 0)
            values(BLOCKS - 1, 1)
            keys(BLOCKS - 1, 1)

            def global_key(j):
                if j == 0:
                    pe.wait_ge(wg_loaded, 16 * 6)
                    transpose_weight(raw["wgq"], 2)
                    pe.wait_ge(prep_dve, DVE_MEAN)
                    pe.wait_ge(v_summed, BLOCKS)
                    for oc in range(C):
                        for cc in range(C):
                            pe.matmul(ps[:, 4, oc:oc + 1], raw["wgk"][:, cc, oc * P:(oc + 1) * P],
                                      xmean[:, cc, 0:1], start=(cc == 0), stop=(cc == C - 1))
                    for cc in range(C):
                        last = pe.matmul(ps[:, 5, 0:D], xmean[:, cc, :], raw["wgv"][:, cc, :],
                                         start=(cc == 0), stop=(cc == C - 1))
                    last.then_inc(prep_pe, 1)
                if j == 2:
                    pe.wait_ge(prep_dve, DVE_GK)
                    for oc in range(C):
                        for cc in range(C):
                            last = pe.matmul(ps[:, 3, oc:oc + 1], wq_t[:, cc, oc * P:(oc + 1) * P],
                                             gk[:, cc:cc + 1], start=(cc == 0), stop=(cc == C - 1))
                    last.then_inc(prep_pe, 1)

            def scores(i, par, j):
                s = 2 * BLOCKS * i + BLOCKS * par + j
                if j == 0:
                    pe.wait_ge(mt_split, 2 * i + par + 1)
                if isinstance(i, int) and i == 0 and par == 0:
                    pe.wait_ge(k_split, j + 1)
                at_least(pe, s_masked, s - 1)
                for cc in range(C):
                    block_keys = slice(j * KEYS, (j + 1) * KEYS)
                    last = three_passes(ps[:, S_BANK + j % 2, :], mt_hi[par][:, cc, :],
                                        mt_lo[par][:, cc, :], kt_hi[:, cc, block_keys],
                                        kt_lo[:, cc, block_keys], cc == 0, cc == C - 1)
                last.then_inc(s_ready, 1)

            def transpose_weights(i, par, g):
                u = 2 * BLOCKS * i + BLOCKS * par + g
                if g in EDGES:
                    piece = EDGES.index(g)
                    pe.wait_ge(exp_ready, PIECES * (2 * i + par) + exps_before(i, par, piece))
                if g >= 2:
                    pe.wait_ge(pt_ready, u - 1)
                else:
                    at_least(pe, pt_ready, u - g - MOVED)
                for k in range(SUB):
                    last = pe.transpose(ps[:, T_BANK + g % 2, k * P:(k + 1) * P],
                                        score[par][:, g * KEYS + k * P:g * KEYS + (k + 1) * P],
                                        ident[:])
                last.then_inc(t_ready, 1)

            def weigh_values(i, par, g):
                u = 2 * BLOCKS * i + BLOCKS * par + g
                pe.wait_ge(pt_ready, u + 1)
                if g == 0:
                    at_least(pe, o_used, 2 * i + par)
                for k in range(SUB):
                    chunk = g * SUB + k
                    w = slice(k * P, (k + 1) * P)
                    pe.matmul(ps[:, O_BANK + par, :], pt_hi[g % 2][:, w], val[:, chunk, :],
                              start=(chunk == 0), stop=False, skip_group_check=True)
                    last = pe.matmul(ps[:, O_BANK + par, 0:D], pt_lo[g % 2][:, w], val[:, chunk, 0:D],
                                     start=False, stop=(chunk == N // P - 1), skip_group_check=True)
                last.then_inc(pv_done, 1)

            def self_values(i, par):
                if isinstance(i, int) and i == 0 and par == 0:
                    pe.wait_ge(prep_dve, PREP_DVE)
                at_least(pe, e_copied, 2 * i + par)
                for cc in range(C):
                    last = three_passes(ps[:, E_BANK, 0:D + 2], mt_hi[par][:, cc, :],
                                        mt_lo[par][:, cc, :], we_hi[:, cc, :], we_lo[:, cc, :],
                                        cc == 0, cc == C - 1)
                last.then_inc(e_ready, 1)

            def slot(i, par, j):
                if exists(i):
                    scores(i, par, j)
                ti, tpar = back(i, par, 1 if j >= 3 else 2)
                if exists(ti) and (j - 3) % BLOCKS < stayed(ti, tpar):
                    transpose_weights(ti, tpar, (j - 3) % BLOCKS)
                vi, vpar = back(i, par, 1 if j >= 4 else 2)
                if exists(vi):
                    weigh_values(vi, vpar, (j - 4) % BLOCKS)
                if isinstance(i, int) and i == 0 and par == 0:
                    global_key(j)
                if j == 4 and exists(i):
                    self_values(i, par)
                if par == 1 and j == 2 and exists(i) and exists(i + 1):
                    transpose_masked_x(i + 1)

            def pair(i):
                for par in range(2):
                    for j in range(BLOCKS):
                        slot(i, par, j)

            pair(0)
            with pe.Fori(1, PAIRS - 1) as i:
                pair(i)
            pair(PAIRS - 1)
            pair(PAIRS)

        @block.scalar
        def _(act):
            def x_hi(b, par):
                act.wait_ge(xt_ready, b + 1)
                at_least(act, k_ready, b - 1)
                for cc in range(C):
                    last = act.activation(xs_hi[par][:, cc, :], ps[:, 2 * par + cc, :], ACT.Copy,
                                          accum_out=xsum[:, cc, bass.ds(b, 1)])
                last.then_inc(xs_hi_ready, 1)

            def v_hi(b, par):
                act.wait_ge(v_summed, b + 1)
                act.activation(val[:, bass.ds(b * SUB, SUB), 0:D], v_sum[:],
                               ACT.Copy).then_inc(v_hi_ready, 1)

            def k_hi(b, par):
                act.wait_ge(k_ready, b + 1)
                act.activation(kt_hi[:, :, bass.ds(b * KEYS, KEYS)], ps[:, M_BANK:M_BANK + 2, :],
                               ACT.Copy).then_inc(k_hi_ready, 1)

            x_hi(0, 0)
            x_hi(1, 1)
            v_hi(0, 0)
            k_hi(0, 0)
            with act.Fori(0, BLOCKS // 2 - 1) as i:
                x_hi(2 * i + 2, 0)
                v_hi(2 * i + 1, 1)
                k_hi(2 * i + 1, 1)
                x_hi(2 * i + 3, 1)
                v_hi(2 * i + 2, 0)
                k_hi(2 * i + 2, 0)
            v_hi(BLOCKS - 1, 1)
            k_hi(BLOCKS - 1, 1)

            def exps(i, par, piece):
                t = 2 * i + par
                if exps_before(i, par, piece) == 1:
                    act.wait_ge(max_ready, t + 1)
                    at_least(act, ev_used, t)
                    act.activation(parts[par][:, PIECES:PIECES + 2], ev[par][:, D:D + 2], ACT.Exp,
                                   bias=neg_max[par][:]).then_inc(ge_ready, 1)
                cols = piece_keys(piece)
                act.activation(score[par][:, cols], score[par][:, cols], ACT.Exp,
                               bias=neg_max[par][:],
                               accum_out=parts[par][:, piece:piece + 1]).then_inc(exp_ready, 1)

            def keep(i, par):
                act.wait_ge(turned_ready, MOVED_PIECES * (2 * i + par + 1))
                for a in range(QUADS):
                    rows = slice(a * B, (a + 1) * B)
                    act.activation(squares(par)[rows, :, a], turned[rows, a], ACT.Copy).then_inc(kept, 1)

            def weights_hi(i, par, g):
                u = 2 * BLOCKS * i + BLOCKS * par + g
                if g < stayed(i, par):
                    act.wait_ge(t_ready, STAYED * (2 * i + par) + g + 1)
                elif g == STAYED:
                    act.wait_ge(moved[par], MOVES * (i + 1))
                    act.wait_ge(kept, QUADS * (2 * i + par + 1))
                at_least(act, pv_done, u - 1)
                act.activation(by_squares(pt_hi[g % 2][:]), transposed(par, g, g < stayed(i, par)),
                               ACT.Copy).then_inc(pt_hi_ready, 1)

            def slot(i, par, j):
                pi, ppar = back(i, par, 1)
                ti, tpar = back(i, par, 1 if j >= 3 else 2)
                if exists(ti):
                    weights_hi(ti, tpar, (j - 3) % BLOCKS)
                if exists(pi):
                    for piece in pieces_in_slot(pi, ppar, j):
                        exps(pi, ppar, piece)
                    if j == 2 and not is_last(pi, ppar):
                        keep(pi, ppar)

            def pair(i):
                for par in range(2):
                    for j in range(BLOCKS):
                        slot(i, par, j)

            pair(0)
            with act.Fori(1, PAIRS - 1) as i:
                pair(i)
            pair(PAIRS - 1)
            pair(PAIRS)

        @block.vector
        def _(dve):
            def split_masked_x(i, par):
                t = 2 * i + par
                mine = ps[:, M_BANK, :].rearrange("p (c n) -> p c n", c=C)[:, :, par * P:(par + 1) * P]
                dve.wait_ge(mt_ready, i + 1)
                if not isinstance(i, int) or i > 0:
                    dve.wait_ge(s_ready, BLOCKS * (t - 1))
                dve.tensor_copy(mt_hi[par][:], mine).then_inc(mt_hi_ready, 1)
                dve.wait_ge(mt_hi_ready, t + 1)
                dve.tensor_tensor(mt_lo[par][:], mine, mt_hi[par][:].bitcast(F32),
                                  ALU.subtract).then_inc(mt_split, 1)

            dve.memset(xtot[:, 0:1], 0.0).then_inc(o_used, 1)
            dve.memset(xtot[:, 1:2], 0.0).then_inc(ev_used, 1)
            dve.memset(gk[:, 0:1], 0.0).then_inc(out_stored, 16)

            steps = [0]

            def step(ins):
                steps[0] += 1
                ins.then_inc(prep_dve, 1)
                dve.wait_ge(prep_dve, steps[0])

            def at(mark):
                assert steps[0] == mark, (steps[0], mark)

            two = "p (c n) -> p c n"
            dve.wait_ge(prep_pe, 1)
            step(dve.tensor_copy(wq_t[:], ps[:, 4, :].rearrange(two, c=C)))
            step(dve.tensor_copy(wk_t[:], ps[:, 5, :].rearrange(two, c=C)))
            at(DVE_WT)
            dve.wait_ge(wv_loaded, 16 * 3)
            step(dve.tensor_copy(wv_hi[:], raw["wlv"][:]))
            step(dve.tensor_tensor(wv_lo[:], raw["wlv"][:], wv_hi[:].bitcast(F32), ALU.subtract))
            at(DVE_WV)

            def x_lo(b, par):
                dve.wait_ge(xs_hi_ready, b + 1)
                dve.tensor_tensor(xs_lo[par][:], ps[:, 2 * par:2 * par + 2, :],
                                  xs_hi[par][:].bitcast(F32), ALU.subtract).then_inc(xs_ready, 1)

            def v_add(b):
                dve.wait_ge(v_ready, b + 1)
                at_least(dve, v_split, b)
                dve.tensor_tensor(v_sum[:].rearrange("p (b a) n -> p b a n", a=2),
                                  ps[:, O_BANK:O_BANK + 2, :].rearrange("p b (a n) -> p b a n", a=2),
                                  blv_all[:].unsqueeze(1).unsqueeze(1).to_broadcast([P, 2, 2, D]),
                                  ALU.add).then_inc(v_summed, 1)

            def v_lo(b):
                dve.wait_ge(v_hi_ready, b + 1)
                chunks = bass.ds(b * SUB, SUB)
                dve.tensor_tensor(val[:, chunks, D:2 * D], v_sum[:], val[:, chunks, 0:D].bitcast(F32),
                                  ALU.subtract).then_inc(v_split, 1)

            def k_lo(b):
                dve.wait_ge(k_hi_ready, b + 1)
                cols = bass.ds(b * KEYS, KEYS)
                dve.tensor_tensor(kt_lo[:, :, cols], ps[:, M_BANK:M_BANK + 2, :],
                                  kt_hi[:, :, cols].bitcast(F32), ALU.subtract).then_inc(k_split, 1)

            x_lo(0, 0)
            dve.wait_ge(prep_pe, 2)
            a_psum = ps[:, 7, :].rearrange(two, c=C)
            step(dve.tensor_scalar(a_hi[:], a_psum, SCALE, None, ALU.mult))
            step(dve.scalar_tensor_tensor(a_lo[:], a_psum, SCALE, a_hi[:].bitcast(F32), ALU.mult,
                                          ALU.subtract))
            at(DVE_A)
            split_masked_x(0, 0)
            split_masked_x(0, 1)
            x_lo(1, 1)
            v_add(0)
            v_lo(0)
            k_lo(0)
            with dve.Fori(0, BLOCKS // 2 - 1) as i:
                x_lo(2 * i + 2, 0)
                v_add(2 * i + 1)
                v_lo(2 * i + 1)
                k_lo(2 * i + 1)
                x_lo(2 * i + 3, 1)
                v_add(2 * i + 2)
                v_lo(2 * i + 2)
                k_lo(2 * i + 2)
            step(dve.tensor_reduce(xtot[:], xsum[:], AX_X, ALU.add))
            for cc in range(C):
                step(dve.tensor_scalar(xmean[:, cc, :], xtot[:, cc:cc + 1].to_broadcast([P, P]),
                                       1.0 / N, None, ALU.mult))
            at(DVE_MEAN)
            v_add(BLOCKS - 1)
            v_lo(BLOCKS - 1)
            k_lo(BLOCKS - 1)

            def global_key(j):
                if j == 1:
                    dve.wait_ge(prep_pe, 3)
                    step(dve.tensor_copy(wq_t[:], ps[:, 2, :].rearrange(two, c=C)))
                    step(dve.tensor_copy(gk[:], ps[:, 4, 0:C]))
                    at(DVE_GK)
                    step(dve.tensor_tensor(gv[:], ps[:, 5, 0:D], bgv_all[:], ALU.add))
                if j == 3:
                    dve.wait_ge(prep_pe, 4)
                    step(dve.tensor_scalar(raw["we"][:, :, D:D + 1], ps[:, 3, 0:C].rearrange(
                        "p (c n) -> p c n", n=1), SCALE, None, ALU.mult))
                    step(dve.tensor_copy(we_hi[:], raw["we"][:]))
                    step(dve.tensor_tensor(we_lo[:], raw["we"][:], we_hi[:].bitcast(F32),
                                           ALU.subtract))
                    at(PREP_DVE)

            def mask_scores(i, par, j):
                s = 2 * BLOCKS * i + BLOCKS * par + j
                dve.wait_ge(s_ready, s + 1)
                if j in EDGES:
                    dve.wait_ge(bias_ready, PIECES * (2 * i + par) + EDGES.index(j) + 1)
                keep_apart(dve)
                mine = score[par][:, j * KEYS:(j + 1) * KEYS]
                dve.tensor_tensor_reduce(mine, ps[:, S_BANK + j % 2, :], mine, 1.0, LOWEST, ALU.add,
                                         ALU.max, ev[par][:, D + 2 + j:D + 3 + j]).then_inc(s_masked, 1)

            def row_max(i, par):
                t = 2 * i + par
                dve.wait_ge(s_masked, BLOCKS * (t + 1))
                dve.wait_ge(e_copied, t + 1)
                dve.tensor_reduce(neg_max[par][:], ev[par][:, D:], AX_X, ALU.max,
                                  negate=True).then_inc(max_ready, 1)

            def add_self_bias(i, par):
                t = 2 * i + par
                dve.wait_ge(e_ready, t + 1)
                at_least(dve, ev_used, t)
                dve.tensor_tensor(ev[par][:, 0:D + 2], ps[:, E_BANK, 0:D + 2], bev_all[:],
                                  ALU.add).then_inc(e_copied, 1)

            def turn_squares(i, par, n):
                t = 2 * i + par
                piece = PIECES - MOVED_PIECES + n
                dve.wait_ge(exp_ready, PIECES * t + exps_before(i, par, piece))
                if n == 0:
                    at_least(dve, kept, QUADS * t)
                    if par == 1:
                        dve.wait_ge(moved[0], MOVES * (i + 1))
                    else:
                        at_least(dve, moved[1], MOVES * i)
                chunks = slice((EDGES[piece] - STAYED) * SUB, (EDGES[piece + 1] - STAYED) * SUB)
                squares_out = turned[:].rearrange("p b h k q -> p b (h k) q")[:, :, chunks, :]
                dve.transpose(squares_out.rearrange("p b k q -> p k b q"),
                              score[par][:, piece_keys(piece)].rearrange(
                                  "p (k b q) -> p k b q", b=QUADS, q=B)).then_inc(turned_ready, 1)

            def weights_lo(i, par, g):
                u = 2 * BLOCKS * i + BLOCKS * par + g
                dve.wait_ge(pt_hi_ready, u + 1)
                dve.tensor_tensor(by_squares(pt_lo[g % 2][:]), transposed(par, g, g < stayed(i, par)),
                                  by_squares(pt_hi[g % 2][:].bitcast(F32)),
                                  ALU.subtract).then_inc(pt_ready, 1)

            def finish(i, par, j):
                t = 2 * i + par
                o = ps[:, O_BANK + par, :]
                m_row, x_row = fin_in[:, 0, :], fin_in[:, 1, :]
                if j == 4:
                    dve.wait_ge(exp_ready, PIECES * (t + 1))
                    dve.tensor_reduce(den[:], parts[par][:], AX_X, ALU.add).then_inc(den_ready, 1)
                    dve.wait_ge(den_ready, t + 1)
                    dve.reciprocal(rden[:], den[:]).then_inc(rden_ready, 1)
                    dve.wait_ge(pv_done, BLOCKS * (t + 1))
                    dve.scalar_tensor_tensor(acc[:], gv[:], parts[par][:, PIECES:PIECES + 1],
                                             o[:, 0:D], ALU.mult, ALU.add).then_inc(gv_added, 1)
                    dve.wait_ge(gv_added, t + 1)
                    dve.tensor_tensor(acc[:], o[:, D:2 * D], acc[:], ALU.add).then_inc(o_used, 1)
                if j == 5:
                    dve.wait_ge(o_used, t + 2)
                    dve.scalar_tensor_tensor(acc[:], ev[par][:, 0:D], parts[par][:, PIECES + 1:PIECES + 2],
                                             acc[:], ALU.mult, ALU.add).then_inc(ev_used, 1)
                    dve.wait_ge(ev_used, t + 2)
                    dve.wait_ge(rden_ready, t + 1)
                    dve.wait_ge(fin_loaded, 32 * (t + 1))
                    dve.scalar_tensor_tensor(acc[:], acc[:], rden[:], m_row, ALU.mult,
                                             ALU.max).then_inc(res_ready, 1)
                    dve.wait_ge(res_ready, t + 1)
                    dve.tensor_tensor(acc[:], acc[:], x_row, ALU.add).then_inc(fin_used, 1)
                if j == 6:
                    dve.wait_ge(fin_used, t + 1)
                    dve.bn_stats(stats[:], acc[:]).then_inc(stats_ready, 1)
                    dve.wait_ge(stats_ready, t + 1)
                    keep_apart(dve)
                    dve.bn_aggr(mean_var[:], stats[:]).then_inc(mean_ready, 1)
                if j == 7:
                    dve.wait_ge(rstd_ready, t + 1)
                    dve.wait_ge(out_stored, 16 * (t + 1))
                    dve.tensor_scalar(y[:], acc[:], mean_var[:, 0:1], rstd[:], ALU.subtract,
                                      ALU.mult).then_inc(y_ready, 1)

            def slot(i, par, j):
                if isinstance(i, int) and i == 0 and par == 0:
                    global_key(j)
                if par == 1 and j == 3 and exists(i) and exists(i + 1):
                    split_masked_x(i + 1, 0)
                if par == 0 and j == 3 and exists(i) and not (isinstance(i, int) and i == 0):
                    split_masked_x(i, 1)
                pi, ppar = back(i, par, 1)
                if j == 1 and exists(pi) and not is_last(pi, ppar):
                    for n in range(MOVED_PIECES):
                        turn_squares(pi, ppar, n)
                ti, tpar = back(i, par, 1 if j >= 3 else 2)
                comes_first = (j - 3) % BLOCKS >= stayed(ti, tpar)
                if exists(ti) and comes_first:
                    weights_lo(ti, tpar, (j - 3) % BLOCKS)
                if exists(i):
                    mask_scores(i, par, j)
                    if j == BLOCKS - 1:
                        row_max(i, par)
                if exists(ti) and not comes_first:
                    weights_lo(ti, tpar, (j - 3) % BLOCKS)
                if j == 6 and exists(i):
                    add_self_bias(i, par)
                fi, fpar = back(i, par, 2)
                if exists(fi):
                    finish(fi, fpar, j)

            def pair(i):
                for par in range(2):
                    for j in range(BLOCKS):
                        slot(i, par, j)

            pair(0)
            with dve.Fori(1, PAIRS - 1) as i:
                pair(i)
            pair(PAIRS - 1)
            pair(PAIRS)


DVE_WT = 2
DVE_WV = 4
DVE_A = 6
DVE_MEAN = 9
DVE_GK = 11
PREP_DVE = 15


_INS = ['x', 'adj', 'L0_gnn_masked_x', 'L0_gnn_Wlq', 'L0_gnn_Wlk', 'L0_gnn_Wlv', 'L0_gnn_blv',
        'L0_gnn_Wgq', 'L0_gnn_Wgk', 'L0_gnn_Wgv', 'L0_gnn_bgv', 'L0_gnn_Wes', 'L0_gnn_Wev', 'L0_gnn_bev']


def kernel(**inputs):
    import numpy as _np
    import concourse.bacc as _bacc
    from concourse import mybir as _mybir
    from concourse.bass_utils import run_bass_kernel_spmd as _run

    nc = _bacc.Bacc("TRN2", target_bir_lowering=False, num_devices=1)
    arrays, args = {}, []
    for name in _INS:
        a = _np.ascontiguousarray(inputs[name])
        arrays[f"in_{name}_dram"] = a
        args.append(nc.dram_tensor(f"in_{name}_dram", a.shape, _mybir.dt.from_np(a.dtype), kind="ExternalInput").ap())
    o = nc.dram_tensor("out_0_dram", (N, D), F32, kind="ExternalOutput").ap()
    gnn_resnorm(nc, *args, o)
    r = _run(nc, [arrays], core_ids=[0])
    return r.results[0]["out_0_dram"]
```
